# Optimizing a Trainium2 kernel written in Bass

```python
import numpy as np
import jax
import jax.numpy as jnp

def _softmax(x, axis=-1):
    return jax.nn.softmax(x, axis=axis)

def _gelu(x):
    return jax.nn.gelu(x, approximate=True)

def _silu(x):
    return jax.nn.silu(x)

def _sigmoid(x):
    return jax.nn.sigmoid(x)

def _layernorm(x, axis=-1, eps=1e-05):
    m = jnp.mean(x, axis=axis, keepdims=True)
    v = jnp.var(x, axis=axis, keepdims=True)
    return (x - m) / jnp.sqrt(v + eps)

def _scatter_add(tgt, idx, src, axis=0):
    return tgt.at[idx].add(src)

def _segment_sum(src, seg, n):
    return jax.ops.segment_sum(src, seg, n)
kernel_name = 'mk_early_fusion_d1_tok_img768_r4_90fc40'

def setup_inputs(seed: int=0):
    np.random.seed(seed)
    _w = jnp.asarray

    def _rec_inputs():
        import jax
        import jax.numpy as jnp
        _rk = jax.random.key(seed)
        x = -0.00016672 + 0.999947 * jax.random.normal(jax.random.fold_in(_rk, 1), (8, 96, 96, 3), jnp.float32)
        txt = 0.000359596 + 1.00025 * jax.random.normal(jax.random.fold_in(_rk, 2), (8, 128, 192), jnp.float32)
        return (x, txt)
    x, txt = _rec_inputs()

    def _L0_tok_setup():
        import jax, jax.numpy as jnp
        import numpy as np
        PATCH = 16
        HIDDEN = 192

        def extract_patches(x, p):
            B, H, W, C = x.shape
            Hp, Wp = (H // p, W // p)
            x = x.reshape(B, Hp, p, Wp, p, C)
            x = x.transpose(0, 1, 3, 2, 4, 5)
            return x.reshape(B, Hp * Wp, p * p * C)
        key = jax.random.key(seed)
        k1, k2, k3, k4, k5 = jax.random.split(key, 5)
        B, H, W, C = (64, 96, 96, 3)
        num_patches = (H // PATCH) ** 2
        patch_dim = PATCH * PATCH * C
        contactMap = jax.random.normal(k1, (B, H, W, C), dtype=jnp.float32)
        W_proj = jax.random.normal(k2, (patch_dim, HIDDEN), dtype=jnp.float32) * (1.0 / np.sqrt(patch_dim))
        b_proj = jnp.zeros((HIDDEN,), dtype=jnp.float32)
        cls_token = jax.random.normal(k3, (1, 1, HIDDEN), dtype=jnp.float32) * 0.05
        pos_embedding = jax.random.normal(k4, (num_patches + 1, HIDDEN), dtype=jnp.float32) * 0.05
        return {'contactMap': contactMap, 'W_proj': W_proj, 'b_proj': b_proj, 'cls_token': cls_token, 'pos_embedding': pos_embedding}
    _L0_tok_all = _L0_tok_setup()
    _L0_tok_in = {k: v for k, v in _L0_tok_all.items() if k in ('W_proj', 'b_proj', 'cls_token', 'pos_embedding')}
    del _L0_tok_all

    def _L0_attn_setup():
        import jax, jax.numpy as jnp
        import numpy as np
        B, S, D = (2, 512, 192)
        H, STRIDE = (12, 8)
        HD = D // H

        def _stride_mask(S, stride, causal):
            i = jnp.arange(S)[:, None]
            j = jnp.arange(S)[None, :]
            strided = j % stride == 0
            if causal:
                strided = strided & (j <= i)
            return strided | (j == i) | (j == i - 1)
        key = jax.random.key(seed)
        k0, k1, k2 = jax.random.split(key, 3)
        x = jax.random.normal(k0, (B, S, D), dtype=jnp.float32)
        qkv_w = jax.random.normal(k1, (3 * D, D), dtype=jnp.float32) * 0.02
        qkv_b = jnp.zeros((3 * D,), dtype=jnp.float32)
        out_w = jax.random.normal(k2, (D, D), dtype=jnp.float32) * 0.02
        out_b = jnp.zeros((D,), dtype=jnp.float32)
        return {'x': x, 'qkv_w': qkv_w, 'qkv_b': qkv_b, 'out_w': out_w, 'out_b': out_b}
    _L0_attn_all = _L0_attn_setup()
    _L0_attn_in = {k: v for k, v in _L0_attn_all.items() if k in ('qkv_w', 'qkv_b', 'out_w', 'out_b')}
    del _L0_attn_all

    def _L0_ffn_setup():
        import jax, jax.numpy as jnp
        import numpy as np
        DEPTH = 11

        def _fff_forward(inputs, weights_in, weights_out, depth=DEPTH):
            B, S, _ = inputs.shape
            n_nodes = weights_in.shape[0]
            max_index = n_nodes - 1
            all_logits = jnp.einsum('bsd,nd->bsn', inputs, weights_in)

            def step(prev_idx, _):
                sel = jnp.clip(prev_idx, 0, max_index)
                logits = jnp.take_along_axis(all_logits, sel[..., None], axis=-1)[..., 0]
                new_idx = jnp.clip(2 * sel + 1 + (logits > 0).astype(sel.dtype), 0, max_index)
                return (new_idx, (logits, new_idx))
            idx0 = jnp.zeros((B, S), dtype=jnp.int32)
            _, (logits_seq, idx_seq) = jax.lax.scan(step, idx0, None, length=depth - 1)
            logits = jnp.concatenate([jnp.zeros((1, B, S), all_logits.dtype), logits_seq], axis=0)
            node_idx = jnp.concatenate([idx0[None], idx_seq], axis=0)
            act = jax.nn.gelu(logits, approximate=False)
            onehot = jax.nn.one_hot(node_idx, n_nodes, dtype=act.dtype)
            coeff = jnp.einsum('dbs,dbsn->bsn', act, onehot)
            return jnp.einsum('bsn,nd->bsd', coeff, weights_out)
        key = jax.random.key(seed)
        k1, k2, k3 = jax.random.split(key, 3)
        B, S, D = (4, 1024, 192)
        n_nodes = 2 * DEPTH - 1
        return {'inputs': jax.random.normal(k1, (B, S, D), dtype=jnp.float32), 'weights_in': jax.random.normal(k2, (n_nodes, D), dtype=jnp.float32), 'weights_out': jax.random.normal(k3, (n_nodes, D), dtype=jnp.float32)}
    _L0_ffn_all = _L0_ffn_setup()
    _L0_ffn_in = {k: v for k, v in _L0_ffn_all.items() if k in ('weights_in', 'weights_out')}
    del _L0_ffn_all
    return {'x': x, 'txt': txt, 'L0_tok_W_proj': _L0_tok_in['W_proj'], 'L0_tok_b_proj': _L0_tok_in['b_proj'], 'L0_tok_cls_token': _L0_tok_in['cls_token'], 'L0_tok_pos_embedding': _L0_tok_in['pos_embedding'], 'L0_attn_qkv_w': _L0_attn_in['qkv_w'], 'L0_attn_qkv_b': _L0_attn_in['qkv_b'], 'L0_attn_out_w': _L0_attn_in['out_w'], 'L0_attn_out_b': _L0_attn_in['out_b'], 'L0_ffn_weights_in': _L0_ffn_in['weights_in'], 'L0_ffn_weights_out': _L0_ffn_in['weights_out']}

def reference(x, txt, L0_tok_W_proj, L0_tok_b_proj, L0_tok_cls_token, L0_tok_pos_embedding, L0_attn_qkv_w, L0_attn_qkv_b, L0_attn_out_w, L0_attn_out_b, L0_ffn_weights_in, L0_ffn_weights_out):
    import jax
    import jax.numpy as jnp

    def _L0_tok_ref(contactMap, W_proj, b_proj, cls_token, pos_embedding):
        import jax, jax.numpy as jnp
        import numpy as np
        PATCH = 16
        HIDDEN = 192

        def extract_patches(x, p):
            B, H, W, C = x.shape
            Hp, Wp = (H // p, W // p)
            x = x.reshape(B, Hp, p, Wp, p, C)
            x = x.transpose(0, 1, 3, 2, 4, 5)
            return x.reshape(B, Hp * Wp, p * p * C)
        B = contactMap.shape[0]
        patches = extract_patches(contactMap, PATCH)
        enc = jnp.einsum('bnd,dh->bnh', patches, W_proj) + b_proj
        cls = jnp.broadcast_to(cls_token.astype(contactMap.dtype), (B, 1, enc.shape[-1]))
        enc = jnp.concatenate([cls, enc], axis=1)
        return enc + pos_embedding

    def _L0_attn_ref(x, qkv_w, qkv_b, out_w, out_b):
        import jax, jax.numpy as jnp
        import numpy as np
        B, S, D = (2, 512, 192)
        H, STRIDE = (12, 8)
        HD = D // H

        def _stride_mask(S, stride, causal):
            i = jnp.arange(S)[:, None]
            j = jnp.arange(S)[None, :]
            strided = j % stride == 0
            if causal:
                strided = strided & (j <= i)
            return strided | (j == i) | (j == i - 1)
        Bx, Sx, Dx = x.shape
        qkv = x @ qkv_w.T + qkv_b
        qkv = qkv.reshape(Bx, Sx, 3, H, HD)
        q, k, v = jnp.transpose(qkv, (2, 0, 3, 1, 4))
        scale = HD ** (-0.5)
        attn = jnp.einsum('bhid,bhjd->bhij', q, k) * scale
        mask = _stride_mask(Sx, STRIDE, True)
        attn = jnp.where(mask[None, None], attn, -jnp.inf)
        a = jax.nn.softmax(attn, axis=-1)
        a = jnp.nan_to_num(a, nan=0.0)
        out = jnp.einsum('bhij,bhjd->bhid', a, v)
        out = jnp.transpose(out, (0, 2, 1, 3)).reshape(Bx, Sx, Dx)
        return out @ out_w.T + out_b

    def _L0_ffn_ref(inputs, weights_in, weights_out):
        import jax, jax.numpy as jnp
        import numpy as np
        DEPTH = 11

        def _fff_forward(inputs, weights_in, weights_out, depth=DEPTH):
            B, S, _ = inputs.shape
            n_nodes = weights_in.shape[0]
            max_index = n_nodes - 1
            all_logits = jnp.einsum('bsd,nd->bsn', inputs, weights_in)

            def step(prev_idx, _):
                sel = jnp.clip(prev_idx, 0, max_index)
                logits = jnp.take_along_axis(all_logits, sel[..., None], axis=-1)[..., 0]
                new_idx = jnp.clip(2 * sel + 1 + (logits > 0).astype(sel.dtype), 0, max_index)
                return (new_idx, (logits, new_idx))
            idx0 = jnp.zeros((B, S), dtype=jnp.int32)
            _, (logits_seq, idx_seq) = jax.lax.scan(step, idx0, None, length=depth - 1)
            logits = jnp.concatenate([jnp.zeros((1, B, S), all_logits.dtype), logits_seq], axis=0)
            node_idx = jnp.concatenate([idx0[None], idx_seq], axis=0)
            act = jax.nn.gelu(logits, approximate=False)
            onehot = jax.nn.one_hot(node_idx, n_nodes, dtype=act.dtype)
            coeff = jnp.einsum('dbs,dbsn->bsn', act, onehot)
            return jnp.einsum('bsn,nd->bsd', coeff, weights_out)
        return _fff_forward(inputs, weights_in, weights_out)
    h = _L0_tok_ref(x, L0_tok_W_proj, L0_tok_b_proj, L0_tok_cls_token, L0_tok_pos_embedding)
    h = jnp.concatenate([h, txt], axis=1)
    h = h + _L0_attn_ref(_layernorm(h, axis=-1), L0_attn_qkv_w, L0_attn_qkv_b, L0_attn_out_w, L0_attn_out_b)
    h = h + _L0_ffn_ref(_layernorm(h, axis=-1), L0_ffn_weights_in, L0_ffn_weights_out)
    return h

_drawn_inputs = setup_inputs


def setup_inputs(seed=0):
    import zlib

    import numpy as np

    out = dict(_drawn_inputs(seed))
    spreads = {'L0_tok_b_proj': (0.0, 0.1), 'L0_attn_qkv_b': (0.0, 0.1), 'L0_attn_out_b': (0.0, 0.1)}
    factors = {}
    for name, (base, spread) in spreads.items():
        noise = np.random.default_rng([zlib.crc32(name.encode()), seed]).standard_normal(out[name].shape)
        drawn = base * np.exp(spread * noise) if base else spread * noise
        out[name] = jnp.asarray(drawn.astype(out[name].dtype))
    for name, factor in factors.items():
        out[name] = (out[name] * factor).astype(out[name].dtype)
    return out
```

```python
from contextlib import ExitStack

import concourse.bass as bass
from concourse import mybir

ALU = mybir.AluOpType
ACT = mybir.ActivationFunctionType
F32 = mybir.dt.float32
BF16 = mybir.dt.bfloat16
AX_X = mybir.AxisListType.X

B = 8
IMG = 37
TXT = 128
S = IMG + TXT
D = 192
H, HD = 12, 16
HALF, HH = D // 2, H // 2
KC = 6
STRIDE = 8
KT = (S + STRIDE - 1) // STRIDE
KI = (IMG + STRIDE - 1) // STRIDE
IB = 3
NODES = 21
EPS = 1e-5
SCALE = HD ** -0.5
SLOTS = 1 + TXT

TILES = ([("txt", b, 1) for b in range(0, 4)] + [("img", 0, 3), ("img", 3, 3), ("img", 6, 2)]
         + [("txt", b, 1) for b in range(4, 8)])
N = len(TILES)
TEXTS = [n for n in range(N) if TILES[n][0] == "txt"]
IMAGES = [n for n in range(N) if TILES[n][0] == "img"]
TEXT_RUNS = [(0, 0, 4), (7, 4, 4)]
TURNS = [(0, 1), (2, 3), (7, 8), (9, 10), (4,), (5,), (6,)]
TAILS = [(0, 8), (8, 11)]
OUT_SETS = [[(0, 1), (2, 3), (4, 5), (6,), (7,)], [(8, 9), (10,)]]
ADDS = [(g, s) for g in range(2) for s in OUT_SETS[g]]


def rows(n):
    kind, _, count = TILES[n]
    return TXT if kind == "txt" else IMG * count


def keys(n):
    kind, _, count = TILES[n]
    return KT if kind == "txt" else KI * count


RANGES = ["x0", "x1", "im"]
PARTS = ["k0", "k1", "v0", "v1", "q0", "q1"]


def qkv(r, parts=PARTS):
    return [("qkv", r, p) for p in parts]


UNITS_FIRST = qkv("x0")
UNITS_SECOND = qkv("im") + qkv("x1", ["k0"])
UNITS_AT = {
    0: qkv("x1", ["k1", "v0"]),
    1: [("vbd", 0, 2), ("vbd", 2, 2)] + qkv("x1", ["v1"]),
    2: qkv("x1", ["q0"]),
    3: [("vbd", 4, 2), ("vbd", 6, 1)] + qkv("x1", ["q1"]),
    5: [("vbd", 7, 2), ("vbd", 9, 2)],
}
UNITS = UNITS_FIRST + UNITS_SECOND + [u for s in sorted(UNITS_AT) for u in UNITS_AT[s]]
STEPS = N + 5
RING = 4


def out_of_bank(unit):
    return UNITS.index(unit) + 1


def vbd_unit(n):
    return [u for u in UNITS if u[0] == "vbd" and u[1] <= n < u[1] + u[2]][0]


def range_of(n):
    kind, first, _ = TILES[n]
    return "im" if kind == "img" else "x0" if first < 4 else "x1"


QK_ORDER = ["x0", "im", "x1"]
SPREAD_ORDER = ["x0", "im", "x1"]


def spreads(n):
    if range_of(n) == "im":
        return 8 + 4
    return 2 * (TILES[n][1] + 1) + (4 if range_of(n) == "x1" else 0)


def normalised(n):
    return sum(2 if TILES[i][0] == "txt" else 3 for i in range(n + 1))


XN_ORDER = TEXTS + IMAGES


def build(nc, xp, wp, emb_rows, emb_sel, txt, wqkv, bqkv, wo, win, wout,
          ident_d, identb_d, mask_txt_d, mask_img_d, mask_end_d, head_cols_d,
          out):
    with ExitStack() as ctx:
        def sb(name, shape, dt=F32):
            return ctx.enter_context(nc.sbuf_tensor(name, shape, dt))

        def sem(name):
            return ctx.enter_context(nc.semaphore(name))

        ident = sb("ident", [128, 128])
        identb = sb("identb", [128, 128], BF16)
        mask_txt = sb("mask_txt", [TXT, H * (KT + 2)], BF16)
        mask_img = sb("mask_img", [IB * IMG, H * (IB * KI + 2)], BF16)
        mask_end = sb("mask_end", [rows(IMAGES[-1]), H * (keys(IMAGES[-1]) + 2)], BF16)
        head_cols = sb("head_cols", [HALF, HH])
        xp_sb = sb("xp_sb", [128, KC, B * IMG])
        wp_sb = sb("wp_sb", [128, KC, D])
        emb_rows_sb = sb("emb_rows_sb", [IMG + 2, D])
        emb_sel_sb = sb("emb_sel_sb", [IMG + 2, B * IMG])
        wqkv_sb = sb("wqkv_sb", [HALF, 2, 6, HALF])
        bqkv_sb = sb("bqkv_sb", [HALF, 6])
        wo_sb = sb("wo_sb", [HALF + 1, 2, D])
        win_sb = sb("win_sb", [HALF, 2, NODES])
        wout_sb = sb("wout_sb", [NODES, D])

        h = sb("h", [128, N, D])
        xn = sb("xn", [128, N, D])
        h2 = sb("h2", [128, N, D])
        st1 = sb("st1", [128, N, 6])
        mv1 = sb("mv1", [128, N, 2])
        rs1 = sb("rs1", [128, N])
        st2 = sb("st2", [128, N, 6])
        mv2 = sb("mv2", [128, N, 2])
        rs2 = sb("rs2", [128, N])
        expo = sb("expo", [128, N])
        xnT_x = sb("xnT_x", [HALF, 2, B, TXT])
        xnT_i = sb("xnT_i", [HALF, 2, B * IMG])
        q_x = sb("q_x", [HALF, 2, B, TXT])
        q_i = sb("q_i", [HALF, 2, B * IMG])
        kv_x = sb("kv_x", [HALF, 4, B, SLOTS])
        kv_i = sb("kv_i", [HALF, 4, 1 + B * IMG])
        qk_x = sb("qk_x", [HALF, 2, 2, B, TXT])
        qk_i = sb("qk_i", [HALF, 2, 2, B * IMG])
        spread_x = sb("spread_x", [HALF, B, 4, HH, KT])
        spread_i = sb("spread_i", [HALF, 4, B, HH, KI])
        vbd = sb("vbd", [HH * KT, N, 2, HALF])
        sc = sb("sc", [128, N, H * (KT + 2)])
        ps = sb("ps", [128, RING, 2, HH * KT])
        pb = sb("pb", [128, RING, 2, D])
        mx = sb("mx", [128, N, H])
        sm = sb("sm", [128, N, H])
        rsm = sb("rsm", [128, N, H])
        pT = sb("pT", [HH * KT, RING, 2, 128])
        band = sb("band", [HALF, RING, 2, 128])
        band2 = sb("band2", [HALF, 2, 2, 128])
        oT = sb("oT", [HALF + 1, RING, 2, 128])
        xcT = sb("xcT", [HALF, RING, 2, 128])
        lg = sb("lg", [128, N, NODES])
        lgs = sb("lgs", [128, N, NODES])
        gl = sb("gl", [128, N, NODES])
        side = sb("side", [128, N, 10, 2])
        on = sb("on", [128, N, NODES])
        co = sb("co", [128, N, NODES])
        deep = sb("deep", [128, N, 11])
        dsum = sb("dsum", [128, N])
        coT = sb("coT", [NODES, N, 128])

        bank = [ctx.enter_context(nc.psum_tensor(f"bank{i}", [128, 512], F32)) for i in range(8)]
        R = bank[0:2]
        B_SC, B_BAND, B_PT, B_PV, B_PROJ, B_FF = bank[2:8]
        B_EMB = [B_PV, B_PROJ, B_FF]
        B_LN = [B_SC, B_BAND, B_PT]

        ld_ident, ld_masks, ld_heads, ld_emb = sem("ld_ident"), sem("ld_masks"), sem("ld_heads"), sem("ld_emb")
        ld_patch = [sem(f"ld_patch{k}") for k in range(KC)]
        ld_txt = [sem(f"ld_txt{i}") for i in range(len(TEXT_RUNS))]
        ld_wqkv, ld_wo, ld_ff = sem("ld_wqkv"), sem("ld_wo"), sem("ld_ff")
        expo_set, pads_set, small_set, ones_set = sem("expo_set"), sem("pads_set"), sem("small_set"), sem("ones_set")
        emb_done, emb_out = sem("emb_done"), sem("emb_out")
        stats1, moments1, eps1, rstd1 = sem("stats1"), sem("moments1"), sem("eps1"), sem("rstd1")
        xn_ready, xnT_psum, xnT_ready = sem("xn_ready"), sem("xnT_psum"), sem("xnT_ready")
        unit_done = sem("unit_done")
        unit_out, befores_set = sem("unit_out"), sem("befores_set")
        qk_ready, spread_ready = sem("qk_ready"), sem("spread_ready")
        sc_psum, max_ready, sc_shifted, sc_exp = sem("sc_psum"), sem("max_ready"), sem("sc_shifted"), sem("sc_exp")
        sum_ready, inv_ready, p_ready = sem("sum_ready"), sem("inv_ready"), sem("p_ready")
        p_psum, pT_ready, band_parts, band_ready = sem("p_psum"), sem("pT_ready"), sem("band_parts"), sem("band_ready")
        pv_psum, oT_ready = sem("pv_psum"), sem("oT_ready")
        proj_psum, h2_ready = sem("proj_psum"), sem("h2_ready")
        stats2, moments2, eps2, rstd2 = sem("stats2"), sem("moments2"), sem("eps2"), sem("rstd2")
        xc_ready, xcT_psum, xcT_ready = sem("xc_ready"), sem("xcT_psum"), sem("xcT_ready")
        lg_psum, lg_ready = sem("lg_psum"), sem("lg_ready")
        lgs_ready, gelu_ready, tree, co_ready = sem("lgs_ready"), sem("gelu_ready"), sem("tree"), sem("co_ready")
        coT_psum, coT_ready = sem("coT_psum"), sem("coT_ready")
        ff_psum, res_ready, stored = sem("ff_psum"), sem("res_ready"), sem("stored")

        def tokens(text, image, n):
            _, first, count = TILES[n]
            if TILES[n][0] == "txt":
                return text[:, first] if len(text.shape) == 3 else text[:, :, first]
            cols = slice(first * IMG, (first + count) * IMG)
            return image[:, cols] if len(image.shape) == 2 else image[:, :, cols]

        def values(n, back):
            _, first, count = TILES[n]
            if TILES[n][0] == "txt":
                return kv_x[:, 2:4, first, 1 - back:1 - back + TXT]
            return kv_i[:, 2:4, 1 - back + first * IMG:1 - back + (first + count) * IMG]

        def strided(view, dims):
            return bass.AP(view.tensor, view.offset, [tuple(view.ap[0])] + [tuple(d) for d in dims])

        def scores(buf, n):
            k = keys(n) + 2
            return buf[0:rows(n), 0:H * k].rearrange("p (h k) -> p h k", h=H)

        def half_heads(view, half, lo, hi):
            return view[:, half * HH:(half + 1) * HH, lo:hi]

        def per_head(view, k):
            return view.unsqueeze(2).broadcast_to([view.shape[0], H, k])

        def two(view, n, cols=128):
            return view[:, 0:2 * cols].rearrange("p (g t) -> p g t", g=2)[:, :, 0:rows(n)]

        def ff_place(n):
            for tiles_of in OUT_SETS:
                for b, tiles in zip((B_SC, B_BAND, B_PT, B_PV, B_PROJ), tiles_of):
                    if n in tiles:
                        return b, D * tiles.index(n)

        block = ctx.enter_context(nc.Block())

        @block.sync
        def _(sp):
            sp.dma_start(wqkv_sb[:, :, :, :], wqkv).then_inc(ld_wqkv, 16)
            sp.dma_start(bqkv_sb[:, :], bqkv).then_inc(ld_wqkv, 16)
            sp.dma_start(emb_rows_sb[:, :], emb_rows).then_inc(ld_emb, 16)
            sp.dma_start(emb_sel_sb[:, :], emb_sel).then_inc(ld_emb, 16)
            for k in range(KC):
                sp.dma_start(xp_sb[:, k, :], xp[:, k, :]).then_inc(ld_patch[k], 16)
                sp.dma_start(wp_sb[:, k, :], wp[:, k, :]).then_inc(ld_patch[k], 16)
            sp.dma_start(wo_sb[:, :, :], wo).then_inc(ld_wo, 16)
            sp.dma_start(win_sb[:, :, :], win).then_inc(ld_ff, 16)
            sp.dma_start(wout_sb[:, :], wout).then_inc(ld_ff, 16)
            for i, (_, tiles) in enumerate(ADDS):
                sp.wait_ge(res_ready, i + 1)
                a, m = tiles[0], rows(tiles[0])
                sp.dma_start(out[0:m, a:a + len(tiles), :], h2[0:m, a:a + len(tiles), :]).then_inc(stored, 16)
            sp.wait_ge(stored, 16 * len(ADDS))

        @block.gpsimd
        def _(pool):
            nc.gpsimd.memset(expo[:, :], -0.5).then_inc(expo_set, 1)
            nc.gpsimd.memset(mv1[:, :, :], 0.0).then_inc(small_set, 1)
            nc.gpsimd.memset(mv2[:, :, :], 0.0).then_inc(small_set, 1)
            nc.gpsimd.memset(lg[:, :, :], 0.0).then_inc(small_set, 1)
            nc.gpsimd.memset(co[:, :, 0:1], 0.0).then_inc(small_set, 1)
            nc.gpsimd.memset(kv_i[:, :, 0:1], 0.0).then_inc(pads_set, 1)
            pool.wait_ge(expo_set, 1)

            def inverse_deviation(rs, mv, tiles, eps_sem, rstd_sem, count):
                nc.gpsimd.tensor_scalar(rs[:, tiles], mv[:, tiles, 1], EPS, None, ALU.add).then_inc(eps_sem, 1)
                pool.wait_ge(eps_sem, count)
                nc.gpsimd.tensor_tensor(rs[:, tiles], rs[:, tiles], expo[:, tiles], ALU.pow).then_inc(rstd_sem, 1)

            for i, (a, _, k) in enumerate(TEXT_RUNS):
                pool.wait_ge(moments1, sum(r[2] for r in TEXT_RUNS[:i + 1]))
                inverse_deviation(rs1, mv1, slice(a, a + k), eps1, rstd1, i + 1)
            for i, n in enumerate(IMAGES):
                pool.wait_ge(moments1, len(TEXTS) + i + 1)
                inverse_deviation(rs1, mv1, slice(n, n + 1), eps1, rstd1, len(TEXT_RUNS) + i + 1)

            def befores():
                pool.wait_ge(unit_out, out_of_bank(("qkv", "im", "v1")))
                nc.gpsimd.tensor_copy(kv_x[:, :, :, 0], kv_i[:, :, IMG::IMG]).then_inc(befores_set, 1)

            def products(r):
                pool.wait_ge(unit_out, out_of_bank(("qkv", r, "q1")))
                for w in range(2):
                    for half in range(2):
                        if r == "im":
                            o, q = qk_i[:, w, half], q_i[:, half]
                            k = kv_i[:, half, 1 - w:1 - w + B * IMG]
                        else:
                            b = 4 * RANGES.index(r)
                            o, q = qk_x[:, w, half, b:b + 4], q_x[:, half, b:b + 4]
                            k = kv_x[:, half, b:b + 4, 1 - w:1 - w + TXT]
                        nc.gpsimd.tensor_tensor(o, q, k, ALU.mult).then_inc(qk_ready, 1)

            def head_mask(m):
                return head_cols[:, :].unsqueeze(1).unsqueeze(3).broadcast_to([HALF, 4, HH, m])

            def spread(r):
                pool.wait_ge(unit_out, out_of_bank(("qkv", r, "v1")))
                if r == "im":
                    for p in range(4):
                        nc.gpsimd.tensor_tensor(
                            spread_i[:, p],
                            strided(kv_i[:, p, 1:2], [(IMG, B), (0, HH), (STRIDE, KI)]),
                            head_cols[:, :].unsqueeze(1).unsqueeze(3).broadcast_to([HALF, B, HH, KI]),
                            ALU.mult).then_inc(spread_ready, 1)
                    return
                plane = 1 + B * IMG
                first_text = STRIDE * KI - IMG
                for b in range(4 * RANGES.index(r), 4 * RANGES.index(r) + 4):
                    nc.gpsimd.tensor_tensor(
                        spread_x[:, b, :, :, 0:KI],
                        strided(kv_i[:, 0, 1 + b * IMG:2 + b * IMG], [(plane, 4), (0, HH), (STRIDE, KI)]),
                        head_mask(KI), ALU.mult).then_inc(spread_ready, 1)
                    nc.gpsimd.tensor_tensor(
                        spread_x[:, b, :, :, KI:KT],
                        strided(kv_x[:, 0, b, 1 + first_text:2 + first_text],
                                [(B * SLOTS, 4), (0, HH), (STRIDE, KT - KI)]),
                        head_mask(KT - KI), ALU.mult).then_inc(spread_ready, 1)

            def normalise(n):
                m, k = rows(n), keys(n)
                pool.wait_ge(inv_ready, n + 1)
                s = scores(sc[:, n, :], n)
                if TILES[n][0] == "txt":
                    nc.gpsimd.tensor_tensor(ps[0:m, n % RING].rearrange("p g (h k) -> p (g h) k", h=HH), s[:, :, 0:k],
                                            per_head(rsm[0:m, n, :], k), ALU.mult).then_inc(p_ready, 1)
                else:
                    b = TILES[n][2]
                    for half in range(2):
                        src = half_heads(s, half, 0, k).rearrange("p h (b k) -> p b h k", b=b)
                        r = rsm[0:m, n, half * HH:(half + 1) * HH].unsqueeze(1).unsqueeze(3)
                        nc.gpsimd.tensor_tensor(
                            ps[0:m, n % RING, half, 0:HH * k].rearrange("p (b h k) -> p b h k", b=b, h=HH), src,
                            r.broadcast_to([m, b, HH, KI]), ALU.mult).then_inc(p_ready, 1)
                src = s[:, :, k:k + 2].rearrange("p h w -> p w h").unsqueeze(3).broadcast_to([m, 2, H, HD])
                r = rsm[0:m, n, :].unsqueeze(1).unsqueeze(3).broadcast_to([m, 2, H, HD])
                nc.gpsimd.tensor_tensor(pb[0:m, n % RING].rearrange("p w (h f) -> p w h f", h=H), src, r,
                                        ALU.mult).then_inc(p_ready, 1)

            def band_sum(n):
                pool.wait_ge(band_parts, 2 * (n + 1))
                nc.gpsimd.tensor_tensor(band[:, n % RING, :, 0:rows(n)], band[:, n % RING, :, 0:rows(n)],
                                        band2[:, n % 2, :, 0:rows(n)], ALU.add).then_inc(band_ready, 1)

            pool.wait_ge(ld_heads, 16)
            pool.wait_ge(pads_set, 1)
            befores()
            pool.wait_ge(befores_set, 1)
            spread("x0")
            products("x0")
            spread("im")
            products("im")
            for s in range(STEPS):
                if s < N:
                    normalise(s)
                if 0 <= s - 1 < N:
                    band_sum(s - 1)
                if s == 2:
                    spread("x1")
                if s == 3:
                    products("x1")
                for g, (lo, hi) in enumerate(TAILS):
                    if s == hi + 2:
                        pool.wait_ge(moments2, hi)
                        inverse_deviation(rs2, mv2, slice(lo, hi), eps2, rstd2, g + 1)

        @block.scalar
        def _(act):
            act.dma_start(ident[:, :], ident_d).then_inc(ld_ident, 16)
            for i, (a, b, k) in enumerate(TEXT_RUNS):
                act.dma_start(h[:, a:a + k, :], txt[:, b:b + k, :]).then_inc(ld_txt[i], 16)
            act.dma_start(head_cols[:, :], head_cols_d).then_inc(ld_heads, 16)
            act.dma_start(identb[:, :], identb_d).then_inc(ld_masks, 16)
            act.dma_start(mask_txt[:, :], mask_txt_d).then_inc(ld_masks, 16)
            act.dma_start(mask_img[:, :], mask_img_d).then_inc(ld_masks, 16)
            act.dma_start(mask_end[:, :], mask_end_d).then_inc(ld_masks, 16)

            def xnT_out(i):
                tiles = TURNS[i]
                n, b = tiles[0], B_LN[i % len(B_LN)]
                act.wait_ge(xnT_psum, i + 1)
                if len(tiles) == 2:
                    first = TILES[n][1]
                    nc.scalar.activation(xnT_x[:, :, first:first + 2, :],
                                         b[0:HALF, :].rearrange("p (b g t) -> p g b t", b=2, g=2),
                                         ACT.Copy).then_inc(xnT_ready, 1)
                else:
                    nc.scalar.activation(tokens(xnT_x, xnT_i, n), two(b[0:HALF, :], n),
                                         ACT.Copy).then_inc(xnT_ready, 1)

            def unit_evict(u):
                what = UNITS[u]
                act.wait_ge(unit_done, u + 1)
                if what[0] == "vbd":
                    _, n, count = what
                    k = HH * keys(n)
                    nc.scalar.activation(vbd[0:k, n:n + count, :, :].rearrange("p t g f -> p (t g f)"),
                                         R[u % 2][0:k, 0:count * D], ACT.Copy).then_inc(unit_out, 1)
                    return
                _, r, p = what
                g = int(p[1])
                part = "qkv".index(p[0]) * 2 + g
                if r == "im":
                    dst = q_i[:, g] if p[0] == "q" else kv_i[:, part - 2, 1:]
                    src = R[u % 2][0:HALF, 0:B * IMG]
                else:
                    b = 4 * RANGES.index(r)
                    dst = q_x[:, g, b:b + 4] if p[0] == "q" else kv_x[:, part - 2, b:b + 4, 1:]
                    src = R[u % 2][0:HALF, :].rearrange("p (b t) -> p b t", b=4)
                nc.scalar.activation(dst, src, ACT.Identity, bias=bqkv_sb[:, part:part + 1]).then_inc(unit_out, 1)

            def evictions(units, base):
                for i in range(len(units)):
                    unit_evict(base + i)

            for i in range(2):
                xnT_out(i)
            act.wait_ge(ld_wqkv, 32)
            evictions(UNITS_FIRST, 0)
            for i in range(2, 4):
                xnT_out(i)
            for i, n in enumerate(IMAGES):
                act.wait_ge(emb_done, i + 1)
                nc.scalar.activation(h[0:rows(n), n, :], B_EMB[i][0:rows(n), 0:D],
                                     ACT.Copy).then_inc(emb_out, 1)
            for i in range(4, len(TURNS)):
                xnT_out(i)

            def exponent(n):
                act.wait_ge(sc_shifted, n + 1)
                s = sc[0:rows(n), n, 0:H * (keys(n) + 2)]
                nc.scalar.activation(s, s, ACT.Exp, scale=SCALE).then_inc(sc_exp, 1)

            def pT_out(n):
                k = HH * keys(n)
                act.wait_ge(p_psum, n + 1)
                nc.scalar.activation(pT[0:k, n % RING, :, 0:rows(n)], two(B_PT[0:k, :], n),
                                     ACT.Copy).then_inc(pT_ready, 1)

            def lg_out(n):
                act.wait_ge(lg_psum, n + 1)
                if n == 0:
                    act.wait_ge(small_set, 4)
                nc.scalar.activation(lg[0:rows(n), n, :], B_FF[0:rows(n), 256:256 + NODES],
                                     ACT.Copy).then_inc(lg_ready, 1)

            def xcT_out(n):
                act.wait_ge(xcT_psum, n + 1)
                nc.scalar.activation(xcT[:, n % RING, :, 0:rows(n)], two(B_FF[0:HALF, :], n),
                                     ACT.Copy).then_inc(xcT_ready, 1)

            def gelu(g):
                lo, hi = TAILS[g]
                act.wait_ge(lgs_ready, g + 1)
                nc.scalar.activation(gl[:, lo:hi, :], lgs[:, lo:hi, :], ACT.Gelu).then_inc(gelu_ready, 1)

            def coT_out(g):
                lo, hi = TAILS[g]
                for i, a in enumerate(range(lo, hi, 4)):
                    b = min(a + 4, hi)
                    act.wait_ge(coT_psum, a // 4 + 1)
                    nc.scalar.activation(coT[:, a:b, :].rearrange("p n t -> p (n t)"),
                                         R[i][0:NODES, 0:(b - a) * 128], ACT.Copy).then_inc(coT_ready, 1)

            base = len(UNITS_FIRST)
            evictions(UNITS_SECOND, base)
            base += len(UNITS_SECOND)
            for s in range(STEPS):
                if s < N:
                    exponent(s)
                units = UNITS_AT.get(s, [])
                evictions(units[:2], base)
                if 0 <= s - 1 < N:
                    pT_out(s - 1)
                evictions(units[2:], base + 2)
                base += len(units)
                if 0 <= s - 5 < N:
                    lg_out(s - 5)
                if 0 <= s - 4 < N:
                    xcT_out(s - 4)
                if s == TAILS[0][1] + 5:
                    gelu(0)
                if s == TAILS[0][1] + 6:
                    coT_out(0)
            gelu(1)
            coT_out(1)

        @block.vector
        def _(dve):
            def moments(src, st, mv, n, stats_sem, moments_sem, count):
                m = rows(n)
                nc.vector.bn_stats(st[0:m, n, :], src[0:m, n, :]).then_inc(stats_sem, 1)
                dve.wait_ge(stats_sem, count)
                nc.vector.bn_aggr(mv[0:m, n, :], st[0:m, n, :]).then_inc(moments_sem, 1)

            def xn_out(n):
                m = rows(n)
                nc.vector.tensor_scalar(xn[0:m, n, :], h[0:m, n, :], mv1[0:m, n, 0:1], rs1[0:m, n:n + 1],
                                        ALU.subtract, ALU.mult).then_inc(xn_ready, 1)

            nc.vector.memset(oT[HALF:HALF + 1, :, :, :], 1.0).then_inc(ones_set, 1)
            dve.wait_ge(small_set, 4)
            done = 0
            for i, (a, _, k) in enumerate(TEXT_RUNS):
                dve.wait_ge(ld_txt[i], 16)
                for n in range(a, a + k):
                    done += 1
                    moments(h, st1, mv1, n, stats1, moments1, done)
            for i, (a, _, k) in enumerate(TEXT_RUNS):
                dve.wait_ge(rstd1, i + 1)
                for n in range(a, a + k):
                    xn_out(n)
            for i, n in enumerate(IMAGES):
                dve.wait_ge(emb_out, i + 1)
                moments(h, st1, mv1, n, stats1, moments1, len(TEXTS) + i + 1)
            for i, n in enumerate(IMAGES):
                dve.wait_ge(rstd1, len(TEXT_RUNS) + i + 1)
                xn_out(n)
            dve.wait_ge(pads_set, 1)

            def shift(n):
                dve.wait_ge(sc_psum, n + 1)
                s = scores(B_SC[:, :], n)
                nc.vector.tensor_reduce(mx[0:rows(n), n, :], s, AX_X, ALU.max).then_inc(max_ready, 1)
                dve.wait_ge(max_ready, n + 1)
                nc.vector.tensor_tensor(scores(sc[:, n, :], n), s, per_head(mx[0:rows(n), n, :], keys(n) + 2),
                                        ALU.subtract).then_inc(sc_shifted, 1)

            def sums(n):
                m = rows(n)
                dve.wait_ge(sc_exp, n + 1)
                nc.vector.tensor_reduce(sm[0:m, n, :], scores(sc[:, n, :], n), AX_X, ALU.add).then_inc(sum_ready, 1)
                dve.wait_ge(sum_ready, n + 1)
                nc.vector.reciprocal(rsm[0:m, n, :], sm[0:m, n, :]).then_inc(inv_ready, 1)

            def band_products(n):
                m = rows(n)
                dve.wait_ge(p_psum, n + 1)
                p = B_BAND[0:HALF, :].rearrange("p (w g t) -> p w g t", w=2, g=2)[:, :, :, 0:m]
                for w, dst in enumerate((band[:, n % RING], band2[:, n % 2])):
                    nc.vector.tensor_tensor(dst[:, :, 0:m], p[:, w], values(n, w),
                                            ALU.mult).then_inc(band_parts, 1)

            def attended(n):
                m = rows(n)
                dve.wait_ge(pv_psum, n + 1)
                dve.wait_ge(band_ready, n + 1)
                nc.vector.tensor_tensor(oT[0:HALF, n % RING, :, 0:m], two(B_PV[0:HALF, :], n), band[:, n % RING, :, 0:m],
                                        ALU.add).then_inc(oT_ready, 1)

            def residual(n):
                m = rows(n)
                dve.wait_ge(proj_psum, n + 1)
                nc.vector.tensor_tensor(h2[0:m, n, :], B_PROJ[0:m, 0:D], h[0:m, n, :],
                                        ALU.add).then_inc(h2_ready, 1)
                dve.wait_ge(h2_ready, n + 1)
                moments(h2, st2, mv2, n, stats2, moments2, n + 1)
                dve.wait_ge(moments2, n + 1)
                nc.vector.tensor_scalar(xn[0:m, n, :], h2[0:m, n, :], mv2[0:m, n, 0:1], None,
                                        ALU.subtract).then_inc(xc_ready, 1)

            ticks = [0]

            def tick(ins):
                ticks[0] += 1
                ins.then_inc(tree, 1)
                dve.wait_ge(tree, ticks[0])

            def scaled_logits(g):
                lo, hi = TAILS[g]
                k = hi - lo
                dve.wait_ge(lg_ready, hi)
                dve.wait_ge(rstd2, g + 1)
                nc.vector.tensor_tensor(lgs[:, lo:hi, :], lg[:, lo:hi, :],
                                        rs2[:, lo:hi].unsqueeze(2).broadcast_to([128, k, NODES]),
                                        ALU.mult).then_inc(lgs_ready, 1)

            def path(g):
                lo, hi = TAILS[g]
                k = hi - lo
                tick(nc.vector.tensor_scalar(side[:, lo:hi, :, 1], lg[:, lo:hi, 0:10], 0.0, None, ALU.is_gt))
                tick(nc.vector.tensor_scalar(side[:, lo:hi, :, 0], side[:, lo:hi, :, 1], -1.0, 1.0,
                                             ALU.mult, ALU.add))
                nc.vector.tensor_copy(on[:, lo:hi, 1:3], side[:, lo:hi, 0, :]).then_inc(tree, 1)
                ticks[0] += 1
                dve.wait_ge(tree, ticks[0])

                def children(first, count, at):
                    parents = on[:, lo:hi, first:first + count].unsqueeze(3).broadcast_to([128, k, count, 2])
                    tick(nc.vector.tensor_tensor(
                        on[:, lo:hi, at:at + 2 * count].rearrange("p t (n s) -> p t n s", s=2),
                        parents, side[:, lo:hi, first:first + count, :], ALU.mult))

                children(1, 2, 3)
                children(3, 4, 7)
                children(7, 3, 15)

            def coefficients(g):
                lo, hi = TAILS[g]
                k = hi - lo
                dve.wait_ge(gelu_ready, g + 1)

                def rows_of(first, count, at):
                    o = co[:, lo:hi, at:at + 2 * count].rearrange("p t (n s) -> p t n s", s=2)
                    p = on[:, lo:hi, at:at + 2 * count].rearrange("p t (n s) -> p t n s", s=2)
                    v = gl[:, lo:hi, first:first + count].unsqueeze(3).broadcast_to([128, k, count, 2])
                    tick(nc.vector.tensor_tensor(o, p, v, ALU.mult))

                rows_of(0, 7, 1)
                rows_of(7, 3, 15)
                tick(nc.vector.tensor_tensor(gl[:, lo:hi, 10:15], gl[:, lo:hi, 10:15],
                                             gl[:, lo:hi, 20:21].broadcast_to([128, k, 5]), ALU.add))
                tick(nc.vector.tensor_tensor(deep[:, lo:hi, :], on[:, lo:hi, 10:21], gl[:, lo:hi, 10:21],
                                             ALU.mult))
                tick(nc.vector.tensor_reduce(dsum[:, lo:hi], deep[:, lo:hi, :], AX_X, ALU.add))
                tick(nc.vector.scalar_tensor_tensor(dsum[:, lo:hi], gl[:, lo:hi, 20], 5.0, dsum[:, lo:hi],
                                                    ALU.mult, ALU.add))
                nc.vector.tensor_tensor(co[:, lo:hi, 20], co[:, lo:hi, 20], dsum[:, lo:hi],
                                        ALU.add).then_inc(co_ready, 1)

            def results(g):
                for i, (gg, tiles) in enumerate(ADDS):
                    if gg != g:
                        continue
                    a, k, m = tiles[0], len(tiles), rows(tiles[0])
                    b, c = ff_place(a)
                    dve.wait_ge(ff_psum, i + 1)
                    nc.vector.tensor_tensor(h2[0:m, a:a + k, :], h2[0:m, a:a + k, :],
                                            b[0:m, c:c + k * D].rearrange("p (t f) -> p t f", t=k),
                                            ALU.add).then_inc(res_ready, 1)

            for s in range(STEPS):
                if s < N:
                    shift(s)
                    sums(s)
                if 0 <= s - 1 < N:
                    band_products(s - 1)
                if 0 <= s - 2 < N:
                    attended(s - 2)
                if 0 <= s - 3 < N:
                    residual(s - 3)
                if s == TAILS[0][1] + 5:
                    scaled_logits(0)
                    path(0)
                if s == TAILS[0][1] + 6:
                    coefficients(0)
            results(0)
            scaled_logits(1)
            path(1)
            coefficients(1)
            results(1)

        @block.tensor
        def _(pe):
            def xn_transposes(i):
                if i >= len(B_LN):
                    pe.wait_ge(xnT_ready, i - len(B_LN) + 1)
                for j, n in enumerate(TURNS[i]):
                    m = rows(n)
                    pe.wait_ge(xn_ready, XN_ORDER.index(n) + 1)
                    o = two(B_LN[i % len(B_LN)][0:HALF, 256 * j:256 * j + 256], n)
                    for half in range(2):
                        last = nc.tensor.transpose(o[:, half, :], xn[0:m, n, half * HALF:(half + 1) * HALF],
                                                   ident[0:m, 0:m])
                last.then_inc(xnT_psum, 1)

            def unit(u):
                what = UNITS[u]
                o = R[u % 2]
                if u >= 2:
                    pe.wait_ge(unit_out, u - 1)
                if what[0] == "qkv":
                    _, r, p = what
                    part = "qkv".index(p[0]) * 2 + int(p[1])
                    for half in range(2):
                        if r == "im":
                            dst, src = o[0:HALF, 0:B * IMG], xnT_i[:, half]
                        else:
                            b = 4 * RANGES.index(r)
                            dst, src = o[0:HALF, :], xnT_x[:, half, b:b + 4].rearrange("p b t -> p (b t)")
                        last = nc.tensor.matmul(dst, wqkv_sb[:, half, part, :], src,
                                                start=(half == 0), stop=(half == 1))
                else:
                    _, n, count = what
                    k = HH * keys(n)
                    pe.wait_ge(spread_ready, spreads(n + count - 1))
                    for i in range(count):
                        for half in range(2):
                            c = i * D + half * HALF
                            last = nc.tensor.transpose(o[0:k, c:c + HALF], block_diagonal(n + i, 2 + half),
                                                       ident[0:HALF, 0:HALF])
                last.then_inc(unit_done, 1)

            def block_diagonal(n, part):
                _, first, count = TILES[n]
                if TILES[n][0] == "txt":
                    return spread_x[:, first, part].rearrange("p h k -> p (h k)")
                return spread_i[:, part, first:first + count].rearrange("p b h k -> p (b h k)")

            pe.wait_ge(ld_ident, 16)
            for i in range(2):
                xn_transposes(i)
            pe.wait_ge(xnT_ready, 2)
            pe.wait_ge(ld_wqkv, 32)
            for u in range(len(UNITS_FIRST)):
                unit(u)
            for i in range(2, 4):
                xn_transposes(i)

            def image_cols(i):
                _, first, _ = TILES[IMAGES[i]]
                return slice(first * IMG, first * IMG + rows(IMAGES[i]))

            pe.wait_ge(ld_emb, 32)
            for i, n in enumerate(IMAGES):
                nc.tensor.matmul(B_EMB[i][0:rows(n), 0:D], emb_sel_sb[:, image_cols(i)], emb_rows_sb[:, :],
                                 start=True, stop=False)
            for k in range(KC):
                pe.wait_ge(ld_patch[k], 32)
                for i, n in enumerate(IMAGES):
                    last = nc.tensor.matmul(B_EMB[i][0:rows(n), 0:D], xp_sb[:, k, image_cols(i)], wp_sb[:, k, :],
                                            start=False, stop=(k == KC - 1))
                    if k == KC - 1:
                        last.then_inc(emb_done, 1)
            for i in range(4, len(TURNS)):
                xn_transposes(i)
            pe.wait_ge(xnT_ready, len(TURNS))
            for u in range(len(UNITS_FIRST), len(UNITS_FIRST) + len(UNITS_SECOND)):
                unit(u)

            def make_scores(n):
                m, k = rows(n), keys(n)
                if n:
                    pe.wait_ge(sc_shifted, n)
                pe.wait_ge(qk_ready, 4 * (QK_ORDER.index(range_of(n)) + 1))
                pe.wait_ge(spread_ready, spreads(n))
                mask = mask_txt if TILES[n][0] == "txt" else mask_img
                if TILES[n][0] == "img" and TILES[n][2] != IB:
                    mask = mask_end
                o = scores(B_SC[:, :], n)
                nc.tensor.matmul(B_SC[0:m, 0:H * (k + 2)], identb[0:m, 0:m], mask[0:m, 0:H * (k + 2)],
                                 start=True, stop=False, skip_group_check=True)
                for half in range(2):
                    dst = half_heads(o, half, 0, k)
                    if TILES[n][0] == "img":
                        dst = dst.rearrange("p h (b k) -> p b h k", k=KI)
                    nc.tensor.matmul(dst, tokens(q_x[:, half], q_i[:, half], n), block_diagonal(n, half),
                                     start=False, stop=False, skip_group_check=True)
                for w in range(2):
                    for half in range(2):
                        last = nc.tensor.matmul(half_heads(o, half, k + w, k + w + 1),
                                                tokens(qk_x[:, w, half], qk_i[:, w, half], n),
                                                head_cols[:, :].unsqueeze(2),
                                                start=False, stop=(w == 1 and half == 1), skip_group_check=True)
                last.then_inc(sc_psum, 1)

            def turn_probabilities(n):
                m, k = rows(n), keys(n)
                pe.wait_ge(p_ready, normalised(n))
                if n:
                    pe.wait_ge(pT_ready, n)
                    pe.wait_ge(band_parts, 2 * n)
                for half in range(2):
                    nc.tensor.transpose(two(B_PT[0:HH * k, :], n)[:, half, :], ps[0:m, n % RING, half, 0:HH * k],
                                        ident[0:m, 0:m])
                bnd = B_BAND[0:HALF, :].rearrange("p (w g t) -> p w g t", w=2, g=2)
                for w in range(2):
                    for half in range(2):
                        last = nc.tensor.transpose(bnd[:, w, half, 0:m],
                                                   pb[0:m, n % RING, w, half * HALF:(half + 1) * HALF], ident[0:m, 0:m])
                last.then_inc(p_psum, 1)

            def weigh_values(n):
                k = HH * keys(n)
                pe.wait_ge(pT_ready, n + 1)
                pe.wait_ge(unit_out, out_of_bank(vbd_unit(n)))
                if n:
                    pe.wait_ge(oT_ready, n)
                for half in range(2):
                    last = nc.tensor.matmul(two(B_PV[0:HALF, :], n)[:, half, :], vbd[0:k, n, half, :],
                                            pT[0:k, n % RING, half, 0:rows(n)], start=True, stop=True)
                last.then_inc(pv_psum, 1)

            def project(n):
                m = rows(n)
                pe.wait_ge(oT_ready, n + 1)
                if n:
                    pe.wait_ge(h2_ready, n)
                for half in range(2):
                    kk = HALF + 1 if half == 0 else HALF
                    last = nc.tensor.matmul(B_PROJ[0:m, 0:D], oT[0:kk, n % RING, half, 0:m], wo_sb[0:kk, half, :],
                                            start=(half == 0), stop=(half == 1))
                last.then_inc(proj_psum, 1)

            def centred_transposes(n):
                m = rows(n)
                pe.wait_ge(xc_ready, n + 1)
                if n:
                    pe.wait_ge(lg_ready, n)
                for half in range(2):
                    last = nc.tensor.transpose(two(B_FF[0:HALF, :], n)[:, half, :],
                                               xn[0:m, n, half * HALF:(half + 1) * HALF], ident[0:m, 0:m])
                last.then_inc(xcT_psum, 1)

            def logits(n):
                m = rows(n)
                pe.wait_ge(xcT_ready, n + 1)
                for half in range(2):
                    last = nc.tensor.matmul(B_FF[0:m, 256:256 + NODES], xcT[:, n % RING, half, 0:m], win_sb[:, half, :],
                                            start=(half == 0), stop=(half == 1))
                last.then_inc(lg_psum, 1)

            def turn_coefficients(g):
                lo, hi = TAILS[g]
                pe.wait_ge(co_ready, g + 1)
                if g:
                    pe.wait_ge(coT_ready, lo // 4)
                for i, a in enumerate(range(lo, hi, 4)):
                    for n in range(a, min(a + 4, hi)):
                        last = nc.tensor.transpose(R[i][0:NODES, (n - a) * 128:(n - a + 1) * 128],
                                                   co[:, n, :], ident[:, :])
                    last.then_inc(coT_psum, 1)

            def tree_output(g):
                for i, (gg, tiles) in enumerate(ADDS):
                    if gg != g:
                        continue
                    if g:
                        pe.wait_ge(res_ready, len(OUT_SETS[0]))
                    for n in tiles:
                        pe.wait_ge(coT_ready, n // 4 + 1)
                        b, c = ff_place(n)
                        last = nc.tensor.matmul(b[0:rows(n), c:c + D], coT[:, n, 0:rows(n)], wout_sb[:, :],
                                                start=True, stop=True)
                    last.then_inc(ff_psum, 1)

            pe.wait_ge(ld_masks, 64)
            base = len(UNITS_FIRST) + len(UNITS_SECOND)
            for s in range(STEPS):
                if s < N:
                    make_scores(s)
                units = UNITS_AT.get(s, [])
                for i in range(min(2, len(units))):
                    unit(base + i)
                if 0 <= s - 1 < N:
                    turn_probabilities(s - 1)
                if 0 <= s - 2 < N:
                    weigh_values(s - 2)
                for i in range(2, len(units)):
                    unit(base + i)
                base += len(units)
                if s == 3:
                    pe.wait_ge(ld_wo, 16)
                    pe.wait_ge(ones_set, 1)
                if 0 <= s - 3 < N:
                    project(s - 3)
                if s == 5:
                    pe.wait_ge(ld_ff, 32)
                if 0 <= s - 5 < N:
                    logits(s - 5)
                if 0 <= s - 4 < N:
                    centred_transposes(s - 4)
                if s == TAILS[0][1] + 6:
                    turn_coefficients(0)
            tree_output(0)
            turn_coefficients(1)
            tree_output(1)


def _constants(np, bf16):
    masked = -1e30

    def score_mask(positions, key_positions):
        m = np.zeros((len(positions), H, len(key_positions) + 2), np.float32)
        for r, (b, i) in enumerate(positions):
            for c, (kb, j) in enumerate(key_positions):
                if kb != b or j > i:
                    m[r, :, c] = masked
            if i % STRIDE == 0:
                m[r, :, -2] = masked
            if i == 0 or (i - 1) % STRIDE == 0:
                m[r, :, -1] = masked
        return m.reshape(len(positions), -1).astype(bf16)

    def image(count):
        return ([(b, i) for b in range(count) for i in range(IMG)],
                [(b, STRIDE * j) for b in range(count) for j in range(KI)])

    return {
        "ident": np.eye(128, dtype=np.float32),
        "identb": np.eye(128).astype(bf16),
        "mask_txt": score_mask([(0, IMG + t) for t in range(TXT)], [(0, STRIDE * j) for j in range(KT)]),
        "mask_img": score_mask(*image(IB)),
        "mask_end": score_mask(*image(TILES[IMAGES[-1]][2])),
        "head_cols": np.kron(np.eye(HH), np.ones((HD, 1))).astype(np.float32),
    }


def kernel(x, txt, L0_tok_W_proj, L0_tok_b_proj, L0_tok_cls_token, L0_tok_pos_embedding,
           L0_attn_qkv_w, L0_attn_qkv_b, L0_attn_out_w, L0_attn_out_b,
           L0_ffn_weights_in, L0_ffn_weights_out):
    import ml_dtypes
    import numpy as np
    import concourse.bacc as bacc
    from concourse.bass_utils import run_bass_kernel_spmd

    side = x.shape[1] // 16
    patches = np.asarray(x).reshape(B, side, 16, side, 16, 3).transpose(2, 4, 5, 0, 1, 3).reshape(16 * 16 * 3, B, IMG - 1)
    xp = np.zeros((KC * 128, B, IMG), np.float32)
    xp[:, :, 1:] = patches
    emb_sel = np.zeros((IMG + 2, B, IMG), np.float32)
    emb_sel[0, :, 1:] = 1.0
    emb_sel[1, :, 0] = 1.0
    emb_sel[2:] = np.eye(IMG, dtype=np.float32)[:, None, :]
    wo = np.zeros((HALF + 1, 2, D), np.float32)
    wo[:HALF] = np.asarray(L0_attn_out_w).T.reshape(2, HALF, D).transpose(1, 0, 2)
    wo[HALF, 0] = np.asarray(L0_attn_out_b)
    arrays = {
        "xp": xp.reshape(KC, 128, B * IMG).transpose(1, 0, 2),
        "wp": np.asarray(L0_tok_W_proj).reshape(KC, 128, D).transpose(1, 0, 2),
        "emb_rows": np.concatenate([np.asarray(L0_tok_b_proj)[None], np.asarray(L0_tok_cls_token)[0],
                                    np.asarray(L0_tok_pos_embedding)]),
        "emb_sel": emb_sel.reshape(IMG + 2, B * IMG),
        "txt": np.asarray(txt).transpose(1, 0, 2),
        "wqkv": np.asarray(L0_attn_qkv_w).T.reshape(2, HALF, 6, HALF).transpose(1, 0, 2, 3),
        "bqkv": np.asarray(L0_attn_qkv_b).reshape(6, HALF).T,
        "wo": wo,
        "win": np.asarray(L0_ffn_weights_in).T.reshape(2, HALF, NODES).transpose(1, 0, 2),
        "wout": np.asarray(L0_ffn_weights_out),
        **_constants(np, ml_dtypes.bfloat16),
    }
    arrays = {f"in_{name}": np.ascontiguousarray(a) for name, a in arrays.items()}
    nc = bacc.Bacc("TRN2", target_bir_lowering=False, num_devices=1)
    aps = [nc.dram_tensor(name, a.shape, mybir.dt.from_np(a.dtype), kind="ExternalInput").ap()
           for name, a in arrays.items()]
    aps.append(nc.dram_tensor("out", (128, N, D), F32, kind="ExternalOutput").ap())
    build(nc, *aps)
    tiles = run_bass_kernel_spmd(nc, [arrays], core_ids=[0]).results[0]["out"]
    result = np.empty((B, S, D), np.float32)
    for n, (kind, first, count) in enumerate(TILES):
        if kind == "txt":
            result[first, IMG:] = tiles[:, n]
        else:
            result[first:first + count, :IMG] = tiles[:rows(n), n].reshape(count, IMG, D)
    return result
```

```python
from contextlib import ExitStack

import concourse.bass as bass
from concourse import mybir

ALU = mybir.AluOpType
ACT = mybir.ActivationFunctionType
F32 = mybir.dt.float32
BF16 = mybir.dt.bfloat16
AX_X = mybir.AxisListType.X

B = 8
IMG = 37
TXT = 128
S = IMG + TXT
D = 192
H, HD = 12, 16
HALF, HH = D // 2, H // 2
KC = 6
STRIDE = 8
KT = (S + STRIDE - 1) // STRIDE
KI = (IMG + STRIDE - 1) // STRIDE
IB = 3
NODES = 21
EPS = 1e-5
SCALE = HD ** -0.5
SLOTS = 1 + TXT

TILES = ([("txt", b, 1) for b in range(0, 4)] + [("img", 0, 3), ("img", 3, 3), ("img", 6, 2)]
         + [("txt", b, 1) for b in range(4, 8)])
N = len(TILES)
PATCH_LOADS = [(0, 1), (1, 2), (2, 4), (4, 6)]
TEXTS = [n for n in range(N) if TILES[n][0] == "txt"]
IMAGES = [n for n in range(N) if TILES[n][0] == "img"]
TEXT_RUNS = [(0, 0, 4), (7, 4, 4)]
TURNS = [(0, 1), (2, 3), (4,), (5,), (6,), (7, 8), (9, 10)]
TAILS = [(0, 7), (7, 10), (10, 11)]
OUT_SETS = [[(0, 1), (2, 3), (4, 5), (6,)], [(7, 8), (9,)], [(10,)]]
ADDS = [(g, s) for g in range(len(TAILS)) for s in OUT_SETS[g]]
ROW_LEVEL5 = NODES
ROW_LEVEL6 = ROW_LEVEL5 + 11
ROW_REST = ROW_LEVEL6 + 5
ROWS = ROW_REST + 1


def rows(n):
    kind, _, count = TILES[n]
    return TXT if kind == "txt" else IMG * count


def keys(n):
    kind, _, count = TILES[n]
    return KT if kind == "txt" else KI * count


RANGES = ["x0", "x1", "im"]
PARTS = ["k0", "k1", "v0", "v1", "q0", "q1"]


def qkv(r, parts=PARTS):
    return [("qkv", r, p) for p in parts]


FRONT = (qkv("x0", ["k0", "k1"]) + [("turn", 2), ("turn", 3), ("turn", 4)] + qkv("x0", ["v0", "v1"])
         + qkv("im", ["k0", "k1", "v0", "v1"]) + [("turn", 5), ("turn", 6)] + qkv("x0", ["q0", "q1"])
         + qkv("im", ["q0", "q1"]))
UNITS_AT = {
    0: qkv("x1", ["k0", "k1"]),
    1: [("vbd", 0, 2), ("vbd", 2, 2)] + qkv("x1", ["v0"]),
    2: qkv("x1", ["v1"]),
    3: qkv("x1", ["q0"]) + [("vbd", 4, 2), ("vbd", 6, 1)],
    4: qkv("x1", ["q1"]),
    6: [("vbd", 7, 2), ("vbd", 9, 2)],
}
UNITS = [u for u in FRONT if u[0] != "turn"] + [u for s in sorted(UNITS_AT) for u in UNITS_AT[s]]
PREPARE_AT = {3: [("spread", 4), ("spread", 5)], 4: [("spread", 6), ("spread", 7)],
              5: [("qk", 0)], 6: [("qk", 1)]}
LAG_VALUES, LAG_PROJECT, LAG_LOGITS = 1, 2, 3
STEPS = N + LAG_LOGITS
RING = 4


def out_of_bank(unit):
    return UNITS.index(unit) + 1


def vbd_unit(n):
    return [u for u in UNITS if u[0] == "vbd" and u[1] <= n < u[1] + u[2]][0]


def range_of(n):
    kind, first, _ = TILES[n]
    return "im" if kind == "img" else "x0" if first < 4 else "x1"


def spreads(n):
    _, first, _ = TILES[n]
    return {"x0": 4 + first + 1, "im": 12, "x1": 12 + 2 * (first - 4 + 1)}[range_of(n)]


def normalised(n):
    return sum(1 if TILES[i][0] == "txt" else 2 for i in range(n + 1))


XN_ORDER = TEXTS + IMAGES


def build(nc, patch_in, emb_in, txt, wqkv, bqkv, wo, win, wout,
          ident_d, identb_d, mask_txt_d, mask_img_d, mask_end_d, head_cols_d,
          out):
    with ExitStack() as ctx:
        def sb(name, shape, dt=F32):
            return ctx.enter_context(nc.sbuf_tensor(name, shape, dt))

        def sem(name):
            return ctx.enter_context(nc.semaphore(name))

        ident = sb("ident", [128, 128])
        identb = sb("identb", [128, 128], BF16)
        mask_txt = sb("mask_txt", [TXT, H * (KT + 2)], BF16)
        mask_img = sb("mask_img", [IB * IMG, H * (IB * KI + 2)], BF16)
        mask_end = sb("mask_end", [rows(IMAGES[-1]), H * (keys(IMAGES[-1]) + 2)], BF16)
        head_cols = sb("head_cols", [HALF, HH])
        patch_sb = sb("patch_sb", [128, KC, B * IMG + D])
        emb_sb = sb("emb_sb", [IMG + 2, B * IMG + D])
        wqkv_sb = sb("wqkv_sb", [HALF, 2, 6, HALF])
        bqkv_sb = sb("bqkv_sb", [HALF, 6])
        wo_sb = sb("wo_sb", [HALF + 1, 2, D])
        win_sb = sb("win_sb", [HALF, 2, NODES])
        wout_sb = sb("wout_sb", [ROWS, D])

        h = sb("h", [128, N, D])
        xn = sb("xn", [128, N, D])
        h2 = sb("h2", [128, N, D])
        st1 = sb("st1", [128, N, 6])
        mv1 = sb("mv1", [128, N, 2])
        rs1 = sb("rs1", [128, N])
        st2 = sb("st2", [128, N, 6])
        mv2 = sb("mv2", [128, N, 2])
        rs2 = sb("rs2", [128, N])
        expo = sb("expo", [128, N])
        xnT_x = sb("xnT_x", [HALF, 2, B, TXT])
        xnT_i = sb("xnT_i", [HALF, 2, B * IMG])
        q_x = sb("q_x", [HALF, 2, B, TXT])
        q_i = sb("q_i", [HALF, 2, B * IMG])
        kv_x = sb("kv_x", [HALF, 4, B, SLOTS])
        kv_i = sb("kv_i", [HALF, 4, 1 + B * IMG])
        qk_x = sb("qk_x", [HALF, 2, 2, B, TXT])
        qk_i = sb("qk_i", [HALF, 2, 2, B * IMG])
        spread_x = sb("spread_x", [HALF, B, 4, HH, KT])
        spread_i = sb("spread_i", [HALF, 4, B, HH, KI])
        vbd = sb("vbd", [HH * KT, N, 2, HALF])
        sc = sb("sc", [128, N, H * (KT + 2)])
        ps = sb("ps", [128, RING, 2, HH * KT])
        bandp = sb("bandp", [128, N, 2, H])
        pb = sb("pb", [128, RING, 2, D])
        mx = sb("mx", [128, N, H])
        sm = sb("sm", [128, N, H])
        rsm = sb("rsm", [128, N, H])
        pT = sb("pT", [HH * KT, RING, 2, 128])
        band = sb("band", [HALF, RING, 2, 128])
        band2 = sb("band2", [HALF, 2, 2, 128])
        oT = sb("oT", [HALF + 1, RING, 2, 128])
        xcT = sb("xcT", [HALF, RING, 2, 128])
        lg = sb("lg", [128, N, NODES])
        gl = sb("gl", [128, N, NODES])
        on = sb("on", [128, N, NODES])
        co = sb("co", [128, N, ROWS])
        coT = sb("coT", [ROWS, N, 128])

        bank = [ctx.enter_context(nc.psum_tensor(f"bank{i}", [128, 512], F32)) for i in range(8)]
        R = bank[0:2]
        B_SC, B_BAND, B_PT, B_PV, B_PROJ, B_FF = bank[2:8]
        B_EMB = [B_PV, B_PROJ, B_FF]
        B_LN = [B_SC, B_BAND, B_PT]

        ld_ident, ld_masks, ld_heads, ld_emb = sem("ld_ident"), sem("ld_masks"), sem("ld_heads"), sem("ld_emb")
        ld_patch = [sem(f"ld_patch{i}") for i in range(len(PATCH_LOADS))]
        ld_txt = [sem(f"ld_txt{i}") for i in range(len(TEXT_RUNS))]
        ld_wqkv, ld_wo, ld_ff = sem("ld_wqkv"), sem("ld_wo"), sem("ld_ff")
        expo_set, pads_set, small_set, ones_set = sem("expo_set"), sem("pads_set"), sem("small_set"), sem("ones_set")
        emb_done, emb_out = sem("emb_done"), sem("emb_out")
        stats1, moments1, eps1, rstd1 = sem("stats1"), sem("moments1"), sem("eps1"), sem("rstd1")
        xn_ready, xnT_psum, xnT_ready = sem("xn_ready"), sem("xnT_psum"), sem("xnT_ready")
        unit_done = sem("unit_done")
        unit_out, befores_set = sem("unit_out"), sem("befores_set")
        qk_ready = {r: sem(f"qk_ready_{r}") for r in RANGES}
        spread_ready = sem("spread_ready")
        sc_psum, max_ready, sc_shifted, sc_exp = sem("sc_psum"), sem("max_ready"), sem("sc_shifted"), sem("sc_exp")
        sum_ready, inv_ready, p_ready = sem("sum_ready"), sem("inv_ready"), sem("p_ready")
        bandp_ready, pb_ready = sem("bandp_ready"), sem("pb_ready")
        p_psum, pT_ready, band_parts, band_ready = sem("p_psum"), sem("pT_ready"), sem("band_parts"), sem("band_ready")
        pv_psum, oT_ready = sem("pv_psum"), sem("oT_ready")
        proj_psum, h2_ready = sem("proj_psum"), sem("h2_ready")
        stats2, moments2, eps2, rstd2 = sem("stats2"), sem("moments2"), sem("eps2"), sem("rstd2")
        xc_ready, xcT_psum, xcT_ready = sem("xc_ready"), sem("xcT_psum"), sem("xcT_ready")
        lg_psum, lg_ready = sem("lg_psum"), sem("lg_ready")
        gelu_ready, tree, co_ready = sem("gelu_ready"), sem("tree"), sem("co_ready")
        coT_psum, coT_ready = sem("coT_psum"), sem("coT_ready")
        ff_psum, res_ready, stored = sem("ff_psum"), sem("res_ready"), sem("stored")

        def tokens(text, image, n):
            _, first, count = TILES[n]
            if TILES[n][0] == "txt":
                return text[:, first] if len(text.shape) == 3 else text[:, :, first]
            cols = slice(first * IMG, (first + count) * IMG)
            return image[:, cols] if len(image.shape) == 2 else image[:, :, cols]

        def values(n, back):
            _, first, count = TILES[n]
            if TILES[n][0] == "txt":
                return kv_x[:, 2:4, first, 1 - back:1 - back + TXT]
            return kv_i[:, 2:4, 1 - back + first * IMG:1 - back + (first + count) * IMG]

        def strided(view, dims):
            return bass.AP(view.tensor, view.offset, [tuple(view.ap[0])] + [tuple(d) for d in dims])

        def scores(buf, n):
            k = keys(n) + 2
            return buf[0:rows(n), 0:H * k].rearrange("p (h k) -> p h k", h=H)

        def half_heads(view, half, lo, hi):
            return view[:, half * HH:(half + 1) * HH, lo:hi]

        def per_head(view, k):
            return view.unsqueeze(2).broadcast_to([view.shape[0], H, k])

        def two(view, n, cols=128):
            return view[:, 0:2 * cols].rearrange("p (g t) -> p g t", g=2)[:, :, 0:rows(n)]

        def ff_place(n):
            for tiles_of, banks in zip(OUT_SETS, ((B_SC, B_PT, B_BAND, R[0]), (B_PV, B_PROJ), (B_FF,))):
                for b, tiles in zip(banks, tiles_of):
                    if n in tiles:
                        return b, D * tiles.index(n)

        def co_banks(g):
            return (R, R[1:2], R[1:2])[g]

        def qk_operands(r, half, w):
            if r == "im":
                return qk_i[:, w, half], q_i[:, half], kv_i[:, half, 1 - w:1 - w + B * IMG]
            b = 4 * RANGES.index(r)
            return (qk_x[:, w, half, b:b + 4], q_x[:, half, b:b + 4], kv_x[:, half, b:b + 4, 1 - w:1 - w + TXT])

        def turned(g):
            return sum((hi - lo + 3) // 4 for lo, hi in TAILS[:g + 1])

        block = ctx.enter_context(nc.Block())

        @block.sync
        def _(sp):
            sp.dma_start(emb_sb[:, :], emb_in).then_inc(ld_emb, 16)
            for i, (a, b) in enumerate(PATCH_LOADS):
                sp.dma_start(patch_sb[:, a:b, :], patch_in[:, a:b, :]).then_inc(ld_patch[i], 16)
            sp.dma_start(wqkv_sb[:, :, :, :], wqkv).then_inc(ld_wqkv, 16)
            sp.dma_start(bqkv_sb[:, :], bqkv).then_inc(ld_wqkv, 16)
            sp.dma_start(wo_sb[:, :, :], wo).then_inc(ld_wo, 16)
            sp.dma_start(win_sb[:, :, :], win).then_inc(ld_ff, 16)
            sp.dma_start(wout_sb[:, :], wout).then_inc(ld_ff, 16)
            for i, (_, tiles) in enumerate(ADDS):
                sp.wait_ge(res_ready, i + 1)
                a, m = tiles[0], rows(tiles[0])
                sp.dma_start(out[0:m, a:a + len(tiles), :], h2[0:m, a:a + len(tiles), :]).then_inc(stored, 16)
            sp.wait_ge(stored, 16 * len(ADDS))

        @block.gpsimd
        def _(pool):
            nc.gpsimd.memset(expo[:, :], -0.5).then_inc(expo_set, 1)
            nc.gpsimd.memset(mv1[:, :, :], 0.0).then_inc(small_set, 1)
            nc.gpsimd.memset(mv2[:, :, :], 0.0).then_inc(small_set, 1)
            nc.gpsimd.memset(lg[:, :, :], 0.0).then_inc(small_set, 1)
            nc.gpsimd.memset(co[:, :, 0:1], 0.0).then_inc(small_set, 1)
            nc.gpsimd.memset(kv_i[:, :, 0:1], 0.0).then_inc(pads_set, 1)
            pool.wait_ge(expo_set, 1)

            def inverse_deviation(rs, mv, tiles, eps_sem, rstd_sem, count):
                nc.gpsimd.tensor_scalar(rs[:, tiles], mv[:, tiles, 1], EPS, None, ALU.add).then_inc(eps_sem, 1)
                pool.wait_ge(eps_sem, count)
                nc.gpsimd.tensor_tensor(rs[:, tiles], rs[:, tiles], expo[:, tiles], ALU.pow).then_inc(rstd_sem, 1)

            for i, (a, _, k) in enumerate(TEXT_RUNS):
                pool.wait_ge(moments1, sum(r[2] for r in TEXT_RUNS[:i + 1]))
                inverse_deviation(rs1, mv1, slice(a, a + k), eps1, rstd1, i + 1)
            for i, n in enumerate(IMAGES):
                pool.wait_ge(moments1, len(TEXTS) + i + 1)
                inverse_deviation(rs1, mv1, slice(n, n + 1), eps1, rstd1, len(TEXT_RUNS) + i + 1)

            def befores():
                pool.wait_ge(unit_out, out_of_bank(("qkv", "im", "v1")))
                nc.gpsimd.tensor_copy(kv_x[:, :, :, 0], kv_i[:, :, IMG::IMG]).then_inc(befores_set, 1)

            def products(r, half):
                pool.wait_ge(unit_out, out_of_bank(("qkv", r, f"q{half}")))
                for w in range(2):
                    o, q, k = qk_operands(r, half, w)
                    nc.gpsimd.tensor_tensor(o, q, k, ALU.mult).then_inc(qk_ready[r], 1)

            def head_mask(m):
                return head_cols[:, :].unsqueeze(1).unsqueeze(3).broadcast_to([HALF, 4, HH, m])

            def spread_images():
                for p in range(4):
                    nc.gpsimd.tensor_tensor(
                        spread_i[:, p],
                        strided(kv_i[:, p, 1:2], [(IMG, B), (0, HH), (STRIDE, KI)]),
                        head_cols[:, :].unsqueeze(1).unsqueeze(3).broadcast_to([HALF, B, HH, KI]),
                        ALU.mult).then_inc(spread_ready, 1)

            def spread_image_keys(b):
                nc.gpsimd.tensor_tensor(
                    spread_x[:, b, :, :, 0:KI],
                    strided(kv_i[:, 0, 1 + b * IMG:2 + b * IMG], [(1 + B * IMG, 4), (0, HH), (STRIDE, KI)]),
                    head_mask(KI), ALU.mult).then_inc(spread_ready, 1)

            def spread_text_keys(b):
                first_text = STRIDE * KI - IMG
                nc.gpsimd.tensor_tensor(
                    spread_x[:, b, :, :, KI:KT],
                    strided(kv_x[:, 0, b, 1 + first_text:2 + first_text],
                            [(B * SLOTS, 4), (0, HH), (STRIDE, KT - KI)]),
                    head_mask(KT - KI), ALU.mult).then_inc(spread_ready, 1)

            def normalise(n):
                m, k = rows(n), keys(n)
                pool.wait_ge(inv_ready, n + 1)
                s = scores(sc[:, n, :], n)
                if TILES[n][0] == "txt":
                    nc.gpsimd.tensor_tensor(ps[0:m, n % RING].rearrange("p g (h k) -> p (g h) k", h=HH), s[:, :, 0:k],
                                            per_head(rsm[0:m, n, :], k), ALU.mult).then_inc(p_ready, 1)
                else:
                    b = TILES[n][2]
                    for half in range(2):
                        src = half_heads(s, half, 0, k).rearrange("p h (b k) -> p b h k", b=b)
                        r = rsm[0:m, n, half * HH:(half + 1) * HH].unsqueeze(1).unsqueeze(3)
                        nc.gpsimd.tensor_tensor(
                            ps[0:m, n % RING, half, 0:HH * k].rearrange("p (b h k) -> p b h k", b=b, h=HH), src,
                            r.broadcast_to([m, b, HH, KI]), ALU.mult).then_inc(p_ready, 1)

            def band_sum(n):
                pool.wait_ge(band_parts, 2 * (n + 1))
                nc.gpsimd.tensor_tensor(band[:, n % RING, :, 0:rows(n)], band[:, n % RING, :, 0:rows(n)],
                                        band2[:, n % 2, :, 0:rows(n)], ALU.add).then_inc(band_ready, 1)

            pool.wait_ge(ld_heads, 16)
            pool.wait_ge(pads_set, 1)
            pool.wait_ge(unit_out, out_of_bank(("qkv", "x0", "v1")))
            for b in range(4):
                spread_text_keys(b)
            befores()
            for b in range(4):
                spread_image_keys(b)
            spread_images()
            for s in range(STEPS):
                if 0 <= s - LAG_VALUES < N:
                    band_sum(s - LAG_VALUES)
                if s < N:
                    normalise(s)
                for what, i in PREPARE_AT.get(s, []):
                    if what == "spread":
                        pool.wait_ge(unit_out, out_of_bank(("qkv", "x1", "v1")))
                        spread_text_keys(i)
                        spread_image_keys(i)
                    else:
                        if i == 0:
                            pool.wait_ge(befores_set, 1)
                        products("x1", i)
                for g, (lo, hi) in enumerate(TAILS):
                    if s == hi - 1 + LAG_PROJECT:
                        pool.wait_ge(moments2, hi)
                        inverse_deviation(rs2, mv2, slice(lo, hi), eps2, rstd2, g + 1)

        @block.scalar
        def _(act):
            act.dma_start(ident[:, :], ident_d).then_inc(ld_ident, 16)
            for i, (a, b, k) in enumerate(TEXT_RUNS):
                act.dma_start(h[:, a:a + k, :], txt[:, b:b + k, :]).then_inc(ld_txt[i], 16)
            act.dma_start(head_cols[:, :], head_cols_d).then_inc(ld_heads, 16)
            act.dma_start(identb[:, :], identb_d).then_inc(ld_masks, 16)
            act.dma_start(mask_txt[:, :], mask_txt_d).then_inc(ld_masks, 16)
            act.dma_start(mask_img[:, :], mask_img_d).then_inc(ld_masks, 16)
            act.dma_start(mask_end[:, :], mask_end_d).then_inc(ld_masks, 16)

            def xnT_out(i):
                tiles = TURNS[i]
                n, b = tiles[0], B_LN[i % len(B_LN)]
                act.wait_ge(xnT_psum, i + 1)
                if len(tiles) == 2:
                    first = TILES[n][1]
                    nc.scalar.activation(xnT_x[:, :, first:first + 2, :],
                                         b[0:HALF, :].rearrange("p (b g t) -> p g b t", b=2, g=2),
                                         ACT.Copy).then_inc(xnT_ready, 1)
                else:
                    nc.scalar.activation(tokens(xnT_x, xnT_i, n), two(b[0:HALF, :], n),
                                         ACT.Copy).then_inc(xnT_ready, 1)

            def unit_evict(u):
                what = UNITS[u]
                act.wait_ge(unit_done, u + 1)
                if what[0] == "vbd":
                    _, n, count = what
                    k = HH * keys(n)
                    nc.scalar.activation(vbd[0:k, n:n + count, :, :].rearrange("p t g f -> p (t g f)"),
                                         R[u % 2][0:k, 0:count * D], ACT.Copy).then_inc(unit_out, 1)
                    return
                _, r, p = what
                g = int(p[1])
                part = "qkv".index(p[0]) * 2 + g
                if r == "im":
                    dst = q_i[:, g] if p[0] == "q" else kv_i[:, part - 2, 1:]
                    src = R[u % 2][0:HALF, 0:B * IMG]
                else:
                    b = 4 * RANGES.index(r)
                    dst = q_x[:, g, b:b + 4] if p[0] == "q" else kv_x[:, part - 2, b:b + 4, 1:]
                    src = R[u % 2][0:HALF, :].rearrange("p (b t) -> p b t", b=4)
                nc.scalar.activation(dst, src, ACT.Identity, bias=bqkv_sb[:, part:part + 1]).then_inc(unit_out, 1)

            def exponent(n):
                act.wait_ge(sc_shifted, n + 1)
                s = sc[0:rows(n), n, 0:H * (keys(n) + 2)]
                nc.scalar.activation(s, s, ACT.Exp, scale=SCALE).then_inc(sc_exp, 1)

            def repeat_band(n):
                m = rows(n)
                act.wait_ge(bandp_ready, n + 1)
                nc.scalar.activation(pb[0:m, n % RING].rearrange("p w (h f) -> p (w h) f", h=H),
                                     bandp[0:m, n].rearrange("p w h -> p (w h)").unsqueeze(2)
                                     .broadcast_to([m, 2 * H, HD]), ACT.Copy).then_inc(pb_ready, 1)

            def pT_out(n):
                k = HH * keys(n)
                act.wait_ge(p_psum, n + 1)
                nc.scalar.activation(pT[0:k, n % RING, :, 0:rows(n)], two(B_PT[0:k, :], n),
                                     ACT.Copy).then_inc(pT_ready, 1)

            def lg_out(n):
                act.wait_ge(lg_psum, n + 1)
                if n == 0:
                    act.wait_ge(small_set, 4)
                nc.scalar.activation(lg[0:rows(n), n, :], B_FF[0:rows(n), 256:256 + NODES],
                                     ACT.Copy).then_inc(lg_ready, 1)

            def xcT_out(n):
                act.wait_ge(xcT_psum, n + 1)
                nc.scalar.activation(xcT[:, n % RING, :, 0:rows(n)], two(B_FF[0:HALF, :], n),
                                     ACT.Copy).then_inc(xcT_ready, 1)

            def gelu(g):
                lo, hi = TAILS[g]
                act.wait_ge(lg_ready, hi)
                act.wait_ge(rstd2, g + 1)
                for n in range(lo, hi):
                    nc.scalar.activation(gl[:, n, :], lg[:, n, :], ACT.Gelu,
                                         scale=rs2[:, n:n + 1]).then_inc(gelu_ready, 1)

            def coT_out(g):
                lo, hi = TAILS[g]
                for i, a in enumerate(range(lo, hi, 4)):
                    b = min(a + 4, hi)
                    act.wait_ge(coT_psum, (turned(g - 1) if g else 0) + i + 1)
                    nc.scalar.activation(coT[:, a:b, :].rearrange("p n t -> p (n t)"),
                                         co_banks(g)[i][0:ROWS, 0:(b - a) * 128], ACT.Copy).then_inc(coT_ready, 1)

            for i in range(2):
                xnT_out(i)
            for i, n in enumerate(IMAGES):
                act.wait_ge(emb_done, i + 1)
                nc.scalar.activation(h[0:rows(n), n, :], B_EMB[i][0:rows(n), 0:D],
                                     ACT.Copy).then_inc(emb_out, 1)
            act.wait_ge(ld_wqkv, 32)
            for u in FRONT:
                if u[0] == "turn":
                    xnT_out(u[1])
                else:
                    unit_evict(UNITS.index(u))
            for s in range(STEPS):
                if 0 <= s - LAG_LOGITS < N:
                    xcT_out(s - LAG_LOGITS)
                if s < N:
                    exponent(s)
                units = UNITS_AT.get(s, [])
                for u in units[:1]:
                    unit_evict(UNITS.index(u))
                if 0 <= s - LAG_VALUES < N:
                    pT_out(s - LAG_VALUES)
                if s < N:
                    repeat_band(s)
                for u in units[1:]:
                    unit_evict(UNITS.index(u))
                if 0 <= s - LAG_LOGITS < N:
                    lg_out(s - LAG_LOGITS)
                for g, (lo, hi) in enumerate(TAILS):
                    if s == max(hi - 1 + LAG_LOGITS, N - 1):
                        gelu(g)
                if s == N + 1:
                    coT_out(0)
            coT_out(1)
            coT_out(2)

        @block.vector
        def _(dve):
            def moments(src, st, mv, n, stats_sem, moments_sem, count):
                m = rows(n)
                nc.vector.bn_stats(st[0:m, n, :], src[0:m, n, :]).then_inc(stats_sem, 1)
                dve.wait_ge(stats_sem, count)
                nc.vector.bn_aggr(mv[0:m, n, :], st[0:m, n, :]).then_inc(moments_sem, 1)

            def xn_out(n):
                m = rows(n)
                nc.vector.tensor_scalar(xn[0:m, n, :], h[0:m, n, :], mv1[0:m, n, 0:1], rs1[0:m, n:n + 1],
                                        ALU.subtract, ALU.mult).then_inc(xn_ready, 1)

            nc.vector.memset(oT[HALF:HALF + 1, :, :, :], 1.0).then_inc(ones_set, 1)
            dve.wait_ge(small_set, 4)
            done = 0
            for i, (a, _, k) in enumerate(TEXT_RUNS):
                dve.wait_ge(ld_txt[i], 16)
                for n in range(a, a + k):
                    done += 1
                    moments(h, st1, mv1, n, stats1, moments1, done)
            for i, (a, _, k) in enumerate(TEXT_RUNS):
                dve.wait_ge(rstd1, i + 1)
                for n in range(a, a + k):
                    xn_out(n)
            for i, n in enumerate(IMAGES):
                dve.wait_ge(emb_out, i + 1)
                moments(h, st1, mv1, n, stats1, moments1, len(TEXTS) + i + 1)
            for i, n in enumerate(IMAGES):
                dve.wait_ge(rstd1, len(TEXT_RUNS) + i + 1)
                xn_out(n)
            dve.wait_ge(pads_set, 1)
            for r in ("x0", "im"):
                for half in range(2):
                    dve.wait_ge(unit_out, out_of_bank(("qkv", r, f"q{half}")))
                    for w in range(2):
                        if w == 1:
                            dve.wait_ge(befores_set, 1)
                        o, q, k = qk_operands(r, half, w)
                        nc.vector.tensor_tensor(o, q, k, ALU.mult).then_inc(qk_ready[r], 1)

            def shift(n):
                dve.wait_ge(sc_psum, n + 1)
                s = scores(B_SC[:, :], n)
                nc.vector.tensor_reduce(mx[0:rows(n), n, :], s, AX_X, ALU.max).then_inc(max_ready, 1)
                dve.wait_ge(max_ready, n + 1)
                nc.vector.tensor_tensor(scores(sc[:, n, :], n), s, per_head(mx[0:rows(n), n, :], keys(n) + 2),
                                        ALU.subtract).then_inc(sc_shifted, 1)

            def sums(n):
                m = rows(n)
                dve.wait_ge(sc_exp, n + 1)
                nc.vector.tensor_reduce(sm[0:m, n, :], scores(sc[:, n, :], n), AX_X, ALU.add).then_inc(sum_ready, 1)
                dve.wait_ge(sum_ready, n + 1)
                nc.vector.reciprocal(rsm[0:m, n, :], sm[0:m, n, :]).then_inc(inv_ready, 1)
                dve.wait_ge(inv_ready, n + 1)
                k = keys(n)
                nc.vector.tensor_tensor(bandp[0:m, n].rearrange("p w h -> p h w"),
                                        scores(sc[:, n, :], n)[:, :, k:k + 2],
                                        per_head(rsm[0:m, n, :], 2), ALU.mult).then_inc(bandp_ready, 1)

            def band_products(n):
                m = rows(n)
                dve.wait_ge(p_psum, n + 1)
                p = B_BAND[0:HALF, :].rearrange("p (w g t) -> p w g t", w=2, g=2)[:, :, :, 0:m]
                for w, dst in enumerate((band[:, n % RING], band2[:, n % 2])):
                    nc.vector.tensor_tensor(dst[:, :, 0:m], p[:, w], values(n, w),
                                            ALU.mult).then_inc(band_parts, 1)

            def attended(n):
                m = rows(n)
                dve.wait_ge(pv_psum, n + 1)
                dve.wait_ge(band_ready, n + 1)
                nc.vector.tensor_tensor(oT[0:HALF, n % RING, :, 0:m], two(B_PV[0:HALF, :], n), band[:, n % RING, :, 0:m],
                                        ALU.add).then_inc(oT_ready, 1)

            def residual(n):
                m = rows(n)
                dve.wait_ge(proj_psum, n + 1)
                nc.vector.tensor_tensor(h2[0:m, n, :], B_PROJ[0:m, 0:D], h[0:m, n, :],
                                        ALU.add).then_inc(h2_ready, 1)
                dve.wait_ge(h2_ready, n + 1)
                moments(h2, st2, mv2, n, stats2, moments2, n + 1)
                dve.wait_ge(moments2, n + 1)
                nc.vector.tensor_scalar(xn[0:m, n, :], h2[0:m, n, :], mv2[0:m, n, 0:1], None,
                                        ALU.subtract).then_inc(xc_ready, 1)

            ticks = [0]

            def tick(ins):
                ticks[0] += 1
                ins.then_inc(tree, 1)
                dve.wait_ge(tree, ticks[0])

            def path(g):
                lo, hi = TAILS[g]
                k = hi - lo
                dve.wait_ge(lg_ready, hi)
                for right, compare in enumerate((ALU.is_le, ALU.is_gt)):
                    nc.vector.tensor_scalar(on[:, lo:hi, 1 + right:21:2], lg[:, lo:hi, 0:10], 0.0, None,
                                            compare).then_inc(tree, 1)
                    ticks[0] += 1
                dve.wait_ge(tree, ticks[0])

                def children(first, count):
                    parents = on[:, lo:hi, first:first + count].unsqueeze(3).broadcast_to([128, k, count, 2])
                    o = on[:, lo:hi, 2 * first + 1:2 * (first + count) + 1].rearrange("p t (n s) -> p t n s", s=2)
                    tick(nc.vector.tensor_tensor(o, o, parents, ALU.mult))

                children(1, 2)
                children(3, 4)
                children(7, 3)

            def coefficients(g):
                lo, hi = TAILS[g]
                k = hi - lo
                dve.wait_ge(gelu_ready, hi)
                if g == 0:
                    dve.wait_ge(small_set, 4)
                nc.vector.tensor_tensor(co[:, lo:hi, 1:21].rearrange("p t (n s) -> p t n s", s=2),
                                        on[:, lo:hi, 1:21].rearrange("p t (n s) -> p t n s", s=2),
                                        gl[:, lo:hi, 0:10].unsqueeze(3).broadcast_to([128, k, 10, 2]),
                                        ALU.mult).then_inc(co_ready, 1)
                nc.vector.tensor_tensor(co[:, lo:hi, ROW_LEVEL5:ROW_LEVEL6], on[:, lo:hi, 10:21], gl[:, lo:hi, 10:21],
                                        ALU.mult).then_inc(co_ready, 1)
                nc.vector.tensor_tensor(co[:, lo:hi, ROW_LEVEL6:ROW_REST], on[:, lo:hi, 10:15],
                                        gl[:, lo:hi, 20:21].broadcast_to([128, k, 5]),
                                        ALU.mult).then_inc(co_ready, 1)
                nc.vector.tensor_scalar(co[:, lo:hi, ROW_REST], gl[:, lo:hi, 20], 5.0, None,
                                        ALU.mult).then_inc(co_ready, 1)

            def results(g):
                for i, (gg, tiles) in enumerate(ADDS):
                    if gg != g:
                        continue
                    a, k, m = tiles[0], len(tiles), rows(tiles[0])
                    b, c = ff_place(a)
                    dve.wait_ge(ff_psum, i + 1)
                    nc.vector.tensor_tensor(h2[0:m, a:a + k, :], h2[0:m, a:a + k, :],
                                            b[0:m, c:c + k * D].rearrange("p (t f) -> p t f", t=k),
                                            ALU.add).then_inc(res_ready, 1)

            for s in range(STEPS):
                if s == N:
                    path(0)
                if s < N:
                    shift(s)
                if 0 <= s - LAG_VALUES < N:
                    band_products(s - LAG_VALUES)
                if s < N:
                    sums(s)
                if 0 <= s - LAG_VALUES < N:
                    attended(s - LAG_VALUES)
                if 0 <= s - LAG_PROJECT < N:
                    residual(s - LAG_PROJECT)
                if s == N:
                    coefficients(0)
            for g in range(1, len(TAILS)):
                path(g)
                coefficients(g)
                results(g - 1)
            results(len(TAILS) - 1)

        @block.tensor
        def _(pe):
            def xn_transposes(i):
                if i >= len(B_LN):
                    pe.wait_ge(xnT_ready, i - len(B_LN) + 1)
                for j, n in enumerate(TURNS[i]):
                    m = rows(n)
                    pe.wait_ge(xn_ready, XN_ORDER.index(n) + 1)
                    o = two(B_LN[i % len(B_LN)][0:HALF, 256 * j:256 * j + 256], n)
                    for half in range(2):
                        last = nc.tensor.transpose(o[:, half, :], xn[0:m, n, half * HALF:(half + 1) * HALF],
                                                   ident[0:m, 0:m])
                last.then_inc(xnT_psum, 1)

            def unit(u):
                what = UNITS[u]
                o = R[u % 2]
                if u >= 2:
                    pe.wait_ge(unit_out, u - 1)
                if what[0] == "qkv":
                    _, r, p = what
                    part = "qkv".index(p[0]) * 2 + int(p[1])
                    pe.wait_ge(xnT_ready, {"x0": 2, "im": 5, "x1": 7}[r])
                    for half in range(2):
                        if r == "im":
                            dst, src = o[0:HALF, 0:B * IMG], xnT_i[:, half]
                        else:
                            b = 4 * RANGES.index(r)
                            dst, src = o[0:HALF, :], xnT_x[:, half, b:b + 4].rearrange("p b t -> p (b t)")
                        last = nc.tensor.matmul(dst, wqkv_sb[:, half, part, :], src,
                                                start=(half == 0), stop=(half == 1))
                else:
                    _, n, count = what
                    k = HH * keys(n)
                    pe.wait_ge(spread_ready, spreads(n + count - 1))
                    for i in range(count):
                        for half in range(2):
                            c = i * D + half * HALF
                            last = nc.tensor.transpose(o[0:k, c:c + HALF], block_diagonal(n + i, 2 + half),
                                                       ident[0:HALF, 0:HALF])
                last.then_inc(unit_done, 1)

            def block_diagonal(n, part):
                _, first, count = TILES[n]
                if TILES[n][0] == "txt":
                    return spread_x[:, first, part].rearrange("p h k -> p (h k)")
                return spread_i[:, part, first:first + count].rearrange("p b h k -> p (b h k)")

            def image_cols(i):
                _, first, _ = TILES[IMAGES[i]]
                return slice(first * IMG, first * IMG + rows(IMAGES[i]))

            pe.wait_ge(ld_emb, 16)
            for i, n in enumerate(IMAGES):
                nc.tensor.matmul(B_EMB[i][0:rows(n), 0:D], emb_sb[:, image_cols(i)], emb_sb[:, B * IMG:],
                                 start=True, stop=False)
            for load, (a, b) in enumerate(PATCH_LOADS):
                if load == len(PATCH_LOADS) - 1:
                    pe.wait_ge(ld_ident, 16)
                    for i in range(2):
                        xn_transposes(i)
                pe.wait_ge(ld_patch[load], 16)
                for k in range(a, b):
                    for i, n in enumerate(IMAGES):
                        last = nc.tensor.matmul(B_EMB[i][0:rows(n), 0:D], patch_sb[:, k, image_cols(i)],
                                                patch_sb[:, k, B * IMG:], start=False, stop=(k == KC - 1))
                        if k == KC - 1:
                            last.then_inc(emb_done, 1)

            pe.wait_ge(ld_wqkv, 32)
            for u in FRONT:
                if u[0] == "turn":
                    xn_transposes(u[1])
                else:
                    unit(UNITS.index(u))

            def make_scores(n):
                m, k = rows(n), keys(n)
                if n:
                    pe.wait_ge(sc_shifted, n)
                pe.wait_ge(qk_ready[range_of(n)], 4)
                pe.wait_ge(spread_ready, spreads(n))
                mask = mask_txt if TILES[n][0] == "txt" else mask_img
                if TILES[n][0] == "img" and TILES[n][2] != IB:
                    mask = mask_end
                o = scores(B_SC[:, :], n)
                nc.tensor.matmul(B_SC[0:m, 0:H * (k + 2)], identb[0:m, 0:m], mask[0:m, 0:H * (k + 2)],
                                 start=True, stop=False, skip_group_check=True)
                for half in range(2):
                    dst = half_heads(o, half, 0, k)
                    if TILES[n][0] == "img":
                        dst = dst.rearrange("p h (b k) -> p b h k", k=KI)
                    nc.tensor.matmul(dst, tokens(q_x[:, half], q_i[:, half], n), block_diagonal(n, half),
                                     start=False, stop=False, skip_group_check=True)
                for w in range(2):
                    for half in range(2):
                        last = nc.tensor.matmul(half_heads(o, half, k + w, k + w + 1),
                                                tokens(qk_x[:, w, half], qk_i[:, w, half], n),
                                                head_cols[:, :].unsqueeze(2),
                                                start=False, stop=(w == 1 and half == 1), skip_group_check=True)
                last.then_inc(sc_psum, 1)

            def turn_probabilities(n):
                m, k = rows(n), keys(n)
                pe.wait_ge(p_ready, normalised(n))
                pe.wait_ge(pb_ready, n + 1)
                if n:
                    pe.wait_ge(pT_ready, n)
                    pe.wait_ge(band_parts, 2 * n)
                for half in range(2):
                    nc.tensor.transpose(two(B_PT[0:HH * k, :], n)[:, half, :], ps[0:m, n % RING, half, 0:HH * k],
                                        ident[0:m, 0:m])
                bnd = B_BAND[0:HALF, :].rearrange("p (w g t) -> p w g t", w=2, g=2)
                for w in range(2):
                    for half in range(2):
                        last = nc.tensor.transpose(bnd[:, w, half, 0:m],
                                                   pb[0:m, n % RING, w, half * HALF:(half + 1) * HALF], ident[0:m, 0:m])
                last.then_inc(p_psum, 1)

            def weigh_values(n):
                k = HH * keys(n)
                pe.wait_ge(pT_ready, n + 1)
                pe.wait_ge(unit_out, out_of_bank(vbd_unit(n)))
                if n:
                    pe.wait_ge(oT_ready, n)
                for half in range(2):
                    last = nc.tensor.matmul(two(B_PV[0:HALF, :], n)[:, half, :], vbd[0:k, n, half, :],
                                            pT[0:k, n % RING, half, 0:rows(n)], start=True, stop=True)
                last.then_inc(pv_psum, 1)

            def project(n):
                m = rows(n)
                pe.wait_ge(oT_ready, n + 1)
                if n:
                    pe.wait_ge(h2_ready, n)
                for half in range(2):
                    kk = HALF + 1 if half == 0 else HALF
                    last = nc.tensor.matmul(B_PROJ[0:m, 0:D], oT[0:kk, n % RING, half, 0:m], wo_sb[0:kk, half, :],
                                            start=(half == 0), stop=(half == 1))
                last.then_inc(proj_psum, 1)

            def centred_transposes(n):
                m = rows(n)
                pe.wait_ge(xc_ready, n + 1)
                if n:
                    pe.wait_ge(lg_ready, n)
                for half in range(2):
                    last = nc.tensor.transpose(two(B_FF[0:HALF, :], n)[:, half, :],
                                               xn[0:m, n, half * HALF:(half + 1) * HALF], ident[0:m, 0:m])
                last.then_inc(xcT_psum, 1)

            def logits(n):
                m = rows(n)
                pe.wait_ge(xcT_ready, n + 1)
                for half in range(2):
                    last = nc.tensor.matmul(B_FF[0:m, 256:256 + NODES], xcT[:, n % RING, half, 0:m], win_sb[:, half, :],
                                            start=(half == 0), stop=(half == 1))
                last.then_inc(lg_psum, 1)

            def turn_coefficients(g):
                lo, hi = TAILS[g]
                pe.wait_ge(co_ready, 4 * (g + 1))
                if g:
                    pe.wait_ge(coT_ready, turned(g - 1))
                for i, a in enumerate(range(lo, hi, 4)):
                    for n in range(a, min(a + 4, hi)):
                        last = nc.tensor.transpose(co_banks(g)[i][0:ROWS, (n - a) * 128:(n - a + 1) * 128],
                                                   co[:, n, :], ident[:, :])
                    last.then_inc(coT_psum, 1)

            def tree_output(g, sets):
                pe.wait_ge(coT_ready, turned(g))
                for tiles in sets:
                    for n in tiles:
                        b, c = ff_place(n)
                        last = nc.tensor.matmul(b[0:rows(n), c:c + D], coT[:, n, 0:rows(n)], wout_sb[:, :],
                                                start=True, stop=True)
                    last.then_inc(ff_psum, 1)

            pe.wait_ge(ld_masks, 64)
            for s in range(STEPS):
                if s < N:
                    make_scores(s)
                if 0 <= s - LAG_LOGITS < N:
                    if s == STEPS - 1:
                        pe.wait_ge(pT_ready, N)
                        pe.wait_ge(band_parts, 2 * N)
                        tree_output(0, OUT_SETS[0][:2])
                    centred_transposes(s - LAG_LOGITS)
                    if s == STEPS - 1:
                        tree_output(0, OUT_SETS[0][2:])
                units = UNITS_AT.get(s, [])
                for u in units[:1]:
                    unit(UNITS.index(u))
                if 0 <= s - LAG_VALUES < N:
                    turn_probabilities(s - LAG_VALUES)
                if 0 <= s - LAG_PROJECT < N:
                    if s == LAG_PROJECT:
                        pe.wait_ge(ld_wo, 16)
                        pe.wait_ge(ones_set, 1)
                    project(s - LAG_PROJECT)
                if 0 <= s - LAG_VALUES < N:
                    weigh_values(s - LAG_VALUES)
                for u in units[1:]:
                    unit(UNITS.index(u))
                if 0 <= s - LAG_LOGITS < N:
                    if s == LAG_LOGITS:
                        pe.wait_ge(ld_ff, 32)
                    logits(s - LAG_LOGITS)
                if s == N + 1:
                    turn_coefficients(0)
            turn_coefficients(1)
            pe.wait_ge(oT_ready, N)
            pe.wait_ge(h2_ready, N)
            tree_output(1, OUT_SETS[1])
            turn_coefficients(2)
            pe.wait_ge(lg_ready, N)
            tree_output(2, OUT_SETS[2])


def _constants(np, bf16):
    masked = -1e30

    def score_mask(positions, key_positions):
        m = np.zeros((len(positions), H, len(key_positions) + 2), np.float32)
        for r, (b, i) in enumerate(positions):
            for c, (kb, j) in enumerate(key_positions):
                if kb != b or j > i:
                    m[r, :, c] = masked
            if i % STRIDE == 0:
                m[r, :, -2] = masked
            if i == 0 or (i - 1) % STRIDE == 0:
                m[r, :, -1] = masked
        return m.reshape(len(positions), -1).astype(bf16)

    def image(count):
        return ([(b, i) for b in range(count) for i in range(IMG)],
                [(b, STRIDE * j) for b in range(count) for j in range(KI)])

    return {
        "ident": np.eye(128, dtype=np.float32),
        "identb": np.eye(128).astype(bf16),
        "mask_txt": score_mask([(0, IMG + t) for t in range(TXT)], [(0, STRIDE * j) for j in range(KT)]),
        "mask_img": score_mask(*image(IB)),
        "mask_end": score_mask(*image(TILES[IMAGES[-1]][2])),
        "head_cols": np.kron(np.eye(HH), np.ones((HD, 1))).astype(np.float32),
    }


def kernel(x, txt, L0_tok_W_proj, L0_tok_b_proj, L0_tok_cls_token, L0_tok_pos_embedding,
           L0_attn_qkv_w, L0_attn_qkv_b, L0_attn_out_w, L0_attn_out_b,
           L0_ffn_weights_in, L0_ffn_weights_out):
    import ml_dtypes
    import numpy as np
    import concourse.bacc as bacc
    from concourse.bass_utils import run_bass_kernel_spmd

    side = x.shape[1] // 16
    patches = np.asarray(x).reshape(B, side, 16, side, 16, 3).transpose(2, 4, 5, 0, 1, 3).reshape(16 * 16 * 3, B, IMG - 1)
    xp = np.zeros((KC * 128, B, IMG), np.float32)
    xp[:, :, 1:] = patches
    emb_sel = np.zeros((IMG + 2, B, IMG), np.float32)
    emb_sel[0, :, 1:] = 1.0
    emb_sel[1, :, 0] = 1.0
    emb_sel[2:] = np.eye(IMG, dtype=np.float32)[:, None, :]
    wo = np.zeros((HALF + 1, 2, D), np.float32)
    wo[:HALF] = np.asarray(L0_attn_out_w).T.reshape(2, HALF, D).transpose(1, 0, 2)
    wo[HALF, 0] = np.asarray(L0_attn_out_b)
    emb_rows = np.concatenate([np.asarray(L0_tok_b_proj)[None], np.asarray(L0_tok_cls_token)[0],
                               np.asarray(L0_tok_pos_embedding)])
    arrays = {
        "patch": np.concatenate([xp.reshape(KC, 128, B * IMG), np.asarray(L0_tok_W_proj).reshape(KC, 128, D)],
                                axis=2).transpose(1, 0, 2),
        "emb": np.concatenate([emb_sel.reshape(IMG + 2, B * IMG), emb_rows], axis=1),
        "txt": np.asarray(txt).transpose(1, 0, 2),
        "wqkv": np.asarray(L0_attn_qkv_w).T.reshape(2, HALF, 6, HALF).transpose(1, 0, 2, 3),
        "bqkv": np.asarray(L0_attn_qkv_b).reshape(6, HALF).T,
        "wo": wo,
        "win": np.asarray(L0_ffn_weights_in).T.reshape(2, HALF, NODES).transpose(1, 0, 2),
        "wout": np.concatenate([np.asarray(L0_ffn_weights_out)]
                               + [np.asarray(L0_ffn_weights_out)[-1:]] * (ROWS - NODES)),
        **_constants(np, ml_dtypes.bfloat16),
    }
    arrays = {f"in_{name}": np.ascontiguousarray(a) for name, a in arrays.items()}
    nc = bacc.Bacc("TRN2", target_bir_lowering=False, num_devices=1)
    aps = [nc.dram_tensor(name, a.shape, mybir.dt.from_np(a.dtype), kind="ExternalInput").ap()
           for name, a in arrays.items()]
    aps.append(nc.dram_tensor("out", (128, N, D), F32, kind="ExternalOutput").ap())
    build(nc, *aps)
    tiles = run_bass_kernel_spmd(nc, [arrays], core_ids=[0]).results[0]["out"]
    result = np.empty((B, S, D), np.float32)
    for n, (kind, first, count) in enumerate(TILES):
        if kind == "txt":
            result[first, IMG:] = tiles[:, n]
        else:
            result[first:first + count, :IMG] = tiles[:rows(n), n].reshape(count, IMG, D)
    return result
```

```python
from contextlib import ExitStack

import concourse.bass as bass
from concourse import mybir

ALU = mybir.AluOpType
ACT = mybir.ActivationFunctionType
F32 = mybir.dt.float32
BF16 = mybir.dt.bfloat16
F32R = mybir.dt.float32r
AX_X = mybir.AxisListType.X

B = 8
IMG = 37
TXT = 128
S = IMG + TXT
D = 192
H, HD = 12, 16
HALF, HH = D // 2, H // 2
KC = 6
STRIDE = 8
KT = (S + STRIDE - 1) // STRIDE
KI = (IMG + STRIDE - 1) // STRIDE
IB = 3
NODES = 21
EPS = 1e-5
SCALE = HD ** -0.5
DX = D + NODES
WX = 3 * D + NODES
SLOTS = 1 + TXT

TILES = ([("txt", b, 1) for b in range(0, 4)] + [("img", 0, 3), ("img", 3, 3), ("img", 6, 2)]
         + [("txt", b, 1) for b in range(4, 8)])
N = len(TILES)
PATCH_LOADS = [(0, 1), (1, 2), (2, 4), (4, 6)]
IMAGES = [n for n in range(N) if TILES[n][0] == "img"]
TEXT_RUNS = [(0, 0, 4), (7, 4, 4)]
RUNS = [(0, 1, 2, 3), (4, 5, 6), (7, 8, 9, 10)]
TURNS = [(0, 1), (2, 3), (4,), (5,), (6,), (7, 8), (9, 10)]
SCALES = [(0, 7), (7, 10), (10, 11)]
TAILS = [(0, 7), (7, 11)]
OUT_SETS = [[(0, 1), (2, 3), (4, 5), (6,)], [(7, 8), (9, 10)]]
ADDS = [(g, s) for g in range(len(TAILS)) for s in OUT_SETS[g]]
BY_VECTOR = [(4, 5), (7, 8)]
ROW_LEVEL5 = NODES
ROW_LEVEL6 = ROW_LEVEL5 + 11
ROW_REST = ROW_LEVEL6 + 5
ROWS = ROW_REST + 1
STACK = 3 * ROWS


def rows(n):
    kind, _, count = TILES[n]
    return TXT if kind == "txt" else IMG * count


def keys(n):
    kind, _, count = TILES[n]
    return KT if kind == "txt" else KI * count


RANGES = ["x0", "x1", "im"]
PIECES = {"k": [("k0", 0, 96), ("k1", 64, 32)],
          "kv": [("k1", 0, 64), ("v0", 0, 64)],
          "v": [("v1", 0, 96), ("v0", 64, 32)],
          "q": [("q0", 0, 96), ("q1", 64, 32)],
          "qn": [("q1", 0, 64)]}
GROUPS = list(PIECES)
LG = PIECES["qn"][0][2]


def half_index(half):
    return "qkv".index(half[0]) * 2 + int(half[1])


def qkv(r, groups=GROUPS):
    return [("qkv", r, g) for g in groups]


FRONT = (qkv("x0", ["k", "kv", "q"]) + [("turn", 2), ("turn", 3), ("turn", 4)] + qkv("x0", ["v"])
         + [("means",)] + qkv("im", ["k", "kv", "v"]) + [("gain",), ("turn", 5), ("turn", 6)] + qkv("x0", ["qn"])
         + qkv("im", ["q", "qn"]) + qkv("x1", ["k"]) + [("dots", 0)])
UNITS_AT = {
    0: qkv("x1", ["kv"]) + [("dots", 1), ("vbd", 0, 2), ("vbd", 2, 2)],
    1: qkv("x1", ["q"]) + [("logits", 0, 4)],
    2: qkv("x1", ["qn"]) + [("logits", 4, 3)],
    3: qkv("x1", ["v"]) + [("vbd", 4, 2)],
    4: [("vbd", 6, 1)],
    5: [("logits", 7, 4)],
    7: [("vbd", 7, 2)],
    9: [("vbd", 9, 2)],
}
for step in range(N - 1):
    if ("dots", step + 1) not in UNITS_AT.setdefault(step, []):
        UNITS_AT[step].append(("dots", step + 1))
UNITS = [u for u in FRONT if u[0] != "turn"] + [u for s in sorted(UNITS_AT) for u in UNITS_AT[s]]
PREPARE_AT = {0: [("qk", "im", 0)], 1: [("qk", "im", 1)], 2: [("qk", "x1", 0)], 3: [("qk", "x1", 1)],
              4: [("spread", 4)], 5: [("spread", 5)], 6: [("spread", 6)], 7: [("spread", 7)]}
LAG_VALUES, LAG_PROJECT = 1, 2
STEPS = N + LAG_PROJECT
VECTOR_READS = ("dots", "means")
WARM_UP = 9
RING = 2


def leading(s):
    return [u for u in UNITS_AT.get(s, [])[:1] if u[0] == "qkv"]


def out_of_bank(unit):
    return sum(1 for u in UNITS[:UNITS.index(unit) + 1] if u[0] not in VECTOR_READS)


def vbd_unit(n):
    return [u for u in UNITS if u[0] == "vbd" and u[1] <= n < u[1] + u[2]][0]


def logits_unit(n):
    return [u for u in UNITS if u[0] == "logits" and u[1] <= n < u[1] + u[2]][0]


def range_of(n):
    kind, first, _ = TILES[n]
    return "im" if kind == "img" else "x0" if first < 4 else "x1"


def spreads(n):
    _, first, _ = TILES[n]
    return {"x0": 4 + first + 1, "im": 12, "x1": 12 + 2 * (first - 4 + 1)}[range_of(n)]


def normalised(n):
    return sum(1 if TILES[i][0] == "txt" else 2 for i in range(n + 1))


def build(nc, patch_in, emb_in, txt, wqkv, bqkv, wo, wo_rows_in, wout,
          ident_d, identb_d, mask_txt_d, mask_img_d, mask_end_d, head_cols_d, parts,
          out):
    with ExitStack() as ctx:
        def sb(name, shape, dt=F32):
            return ctx.enter_context(nc.sbuf_tensor(name, shape, dt))

        def sem(name):
            return ctx.enter_context(nc.semaphore(name))

        ident = sb("ident", [128, 128])
        identb = sb("identb", [128, 128], BF16)
        mask_txt = sb("mask_txt", [TXT, H * (KT + 2)], BF16)
        mask_img = sb("mask_img", [IB * IMG, H * (IB * KI + 2)], BF16)
        mask_end = sb("mask_end", [rows(IMAGES[-1]), H * (keys(IMAGES[-1]) + 2)], BF16)
        head_cols = sb("head_cols", [HALF, HH])
        patch_sb = sb("patch_sb", [128, KC, B * IMG + D])
        emb_sb = sb("emb_sb", [IB * IMG, 2, D])
        wqkv_sb = sb("wqkv_sb", [HALF, 2, WX])
        wqkv_hi = sb("wqkv_hi", [HALF, 2, WX], F32R)
        wqkv_lo = sb("wqkv_lo", [HALF, 2, WX], F32R)
        bqkv_sb = sb("bqkv_sb", [128, len(GROUPS)])
        wo_sb = sb("wo_sb", [HALF + 1, 2, DX])
        wo_rows = sb("wo_rows", [HALF, 2, 2, HALF + 1])
        win_centred = sb("win_centred", [HALF, 2, NODES])
        average = sb("average", [HALF, HALF])
        wout_sb = sb("wout_sb", [STACK, D])
        wout_hi = sb("wout_hi", [STACK, D], F32R)
        wout_lo = sb("wout_lo", [STACK, D])
        parts_sb = sb("parts_sb", [STACK, 2])
        wout_mix = sb("wout_mix", [STACK, D])
        wout_stack = sb("wout_stack", [STACK, D], F32R)
        ident_r = sb("ident_r", [128, 128], F32R)

        idle = sb("idle", [128, 256], BF16)

        h = sb("h", [128, N, DX])
        xn = sb("xn", [128, N, D])
        h2 = sb("h2", [128, N, DX])
        st1 = sb("st1", [128, N, 6])
        mv1 = sb("mv1", [128, N, 2])
        rs1 = sb("rs1", [128, N])
        dev1 = sb("dev1", [128, N])
        st2 = sb("st2", [128, N, 6])
        mv2 = sb("mv2", [128, N, 2])
        rs2 = sb("rs2", [128, N])
        expo = sb("expo", [128, N])
        xnT_x = [sb(f"xnT_x_{part}", [HALF, 2, B, TXT], F32R) for part in ("hi", "lo")]
        xnT_i = [sb(f"xnT_i_{part}", [HALF, 2, B * IMG], F32R) for part in ("hi", "lo")]
        lgT_x = sb("lgT_x", [LG + NODES, B, TXT])
        lgT_i = sb("lgT_i", [LG + NODES, B * IMG])
        q_x = sb("q_x", [HALF, 2, B, TXT])
        q_i = sb("q_i", [HALF, 2, B * IMG])
        kv_x = sb("kv_x", [HALF, 4, B, SLOTS])
        kv_i = sb("kv_i", [HALF, 4, 1 + B * IMG])
        qk_x = sb("qk_x", [HALF, 2, 2, B, TXT])
        qk_i = sb("qk_i", [HALF, 2, 2, B * IMG])
        spread_x = sb("spread_x", [HALF, B, 4, HH, KT])
        spread_i = sb("spread_i", [HALF, 4, B, HH, KI])
        vbd = sb("vbd", [HH * KT, N, 2, HALF])
        sc = sb("sc", [128, RING, H * (KT + 2)])
        ps = sb("ps", [128, RING, 2, HH * KT])
        bandp = sb("bandp", [128, N, 2, H])
        pb = sb("pb", [128, RING, 2, D])
        mx = sb("mx", [128, N, H])
        sm = sb("sm", [128, N, H])
        rsm = sb("rsm", [128, N, H])
        pT = sb("pT", [HH * KT, RING, 2, 128])
        dots = sb("dots", [128, N, 2, H])
        bandv = sb("bandv", [HALF, RING, 2, 2, 128])
        oT = sb("oT", [HALF + 1, RING, 2, 128])
        gl = sb("gl", [128, N, NODES])
        on = sb("on", [128, N, NODES])
        co = sb("co", [128, N, ROWS])
        co_stack = sb("co_stack", [128, N, 3, ROWS], F32R)
        coT = sb("coT", [STACK, N, 128], F32R)

        bank = [ctx.enter_context(nc.psum_tensor(f"bank{i}", [128, 512], F32)) for i in range(8)]
        R = bank[0:3]
        B_SC, B_BAND, B_PT, B_PV, B_PROJ = bank[3:8]
        B_EMB = [B_PV, B_PROJ, R[2]]
        B_LN = [B_SC, B_BAND, B_PT]

        ld_ident, ld_masks, ld_heads, ld_emb = sem("ld_ident"), sem("ld_masks"), sem("ld_heads"), sem("ld_emb")
        ld_patch = [sem(f"ld_patch{i}") for i in range(len(PATCH_LOADS))]
        ld_txt = [sem(f"ld_txt{i}") for i in range(len(TEXT_RUNS))]
        ld_wqkv, ld_wo, ld_ff = sem("ld_wqkv"), sem("ld_wo"), sem("ld_ff")
        expo_set, pads_set, small_set = sem("expo_set"), sem("pads_set"), sem("small_set")
        ones_set, idle_set = sem("ones_set"), sem("idle_set")
        emb_done, emb_summed, emb_out = sem("emb_done"), sem("emb_summed"), sem("emb_out")
        stats1, moments1, eps1, rstd1 = sem("stats1"), sem("moments1"), sem("eps1"), sem("rstd1")
        w_hi, w_lo = sem("w_hi"), sem("w_lo")
        xn_ready, xnT_psum = sem("xn_ready"), sem("xnT_psum")
        xnT_hi, xnT_lo = sem("xnT_hi"), sem("xnT_lo")
        unit_done = sem("unit_done")
        unit_out, befores_set = sem("unit_out"), sem("befores_set")
        dots_ready, dots_added = sem("dots_ready"), sem("dots_added")
        qk_ready = {r: sem(f"qk_ready_{r}") for r in RANGES}
        spread_ready = sem("spread_ready")
        sc_psum, max_ready, sc_shifted, sc_exp = sem("sc_psum"), sem("max_ready"), sem("sc_shifted"), sem("sc_exp")
        sum_ready, inv_ready, p_ready = sem("sum_ready"), sem("inv_ready"), sem("p_ready")
        bandp_ready, pb_ready = sem("bandp_ready"), sem("pb_ready")
        p_psum, pT_ready, band_parts, band_ready = sem("p_psum"), sem("pT_ready"), sem("band_parts"), sem("band_ready")
        pv_psum, oT_ready = sem("pv_psum"), sem("oT_ready")
        proj_psum, h2_ready = sem("proj_psum"), sem("h2_ready")
        stats2, moments2, eps2, rstd2 = sem("stats2"), sem("moments2"), sem("eps2"), sem("rstd2")
        centred, average_set, dev_ready = sem("centred"), sem("average_set"), sem("dev_ready")
        gelu_ready, tree, co_ready = sem("gelu_ready"), sem("tree"), sem("co_ready")
        co_parts, co_high = sem("co_parts"), sem("co_high")
        kept = sem("kept")
        wout_split, wout_ready, ident_r_set = sem("wout_split"), sem("wout_ready"), sem("ident_r_set")
        coT_psum, coT_ready = sem("coT_psum"), sem("coT_ready")
        ff_psum, res_ready, stored = sem("ff_psum"), sem("res_ready"), sem("stored")

        def tokens(text, image, n):
            _, first, count = TILES[n]
            if TILES[n][0] == "txt":
                return text[:, first] if len(text.shape) == 3 else text[:, :, first]
            cols = slice(first * IMG, (first + count) * IMG)
            return image[:, cols] if len(image.shape) == 2 else image[:, :, cols]

        def turned_tokens(i, part):
            tiles = TURNS[i]
            n, b = tiles[0], B_LN[i % len(B_LN)][0:HALF, :]
            if len(tiles) == 2:
                first = TILES[n][1]
                return xnT_x[part][:, :, first:first + 2, :], b.rearrange("p (b g t) -> p g b t", b=2, g=2)
            return tokens(xnT_x[part], xnT_i[part], n), two(b, n)

        def strided(view, dims):
            return bass.AP(view.tensor, view.offset, [tuple(view.ap[0])] + [tuple(d) for d in dims])

        def values(n):
            _, first, _ = TILES[n]
            if TILES[n][0] == "txt":
                return strided(kv_x[:, 2, first, 0:1], [(1, 2), (B * SLOTS, 2), (1, TXT)])
            return strided(kv_i[:, 2, first * IMG:first * IMG + 1], [(1, 2), (1 + B * IMG, 2), (1, rows(n))])

        def scores(buf, n):
            k = keys(n) + 2
            return buf[0:rows(n), 0:H * k].rearrange("p (h k) -> p h k", h=H)

        def half_heads(view, half, lo, hi):
            return view[:, half * HH:(half + 1) * HH, lo:hi]

        def per_head(view, k):
            return view.unsqueeze(2).broadcast_to([view.shape[0], H, k])

        def two(view, n, cols=128):
            return view[:, 0:2 * cols].rearrange("p (g t) -> p g t", g=2)[:, :, 0:rows(n)]

        def ff_place(n):
            for tiles_of, banks in zip(OUT_SETS, ((B_SC, B_PT, B_BAND, R[2]), (B_PV, B_PROJ))):
                for b, tiles in zip(banks, tiles_of):
                    if n in tiles:
                        return b, D * tiles.index(n)

        def co_banks(g):
            return (R[0:2], R[1:2])[g]

        def qk_operands(r, half, w):
            if r == "im":
                return qk_i[:, w, half], q_i[:, half], kv_i[:, half, 1 - w:1 - w + B * IMG]
            b = 4 * RANGES.index(r)
            return (qk_x[:, w, half, b:b + 4], q_x[:, half, b:b + 4], kv_x[:, half, b:b + 4, 1 - w:1 - w + TXT])

        def coefficient_parts(g):
            lo, hi = TAILS[g]
            return (co_stack[:, lo:hi, 0:3:2, :], co_stack[:, lo:hi, 1, :],
                    co[:, lo:hi, :].unsqueeze(2).broadcast_to([128, hi - lo, 2, ROWS]))

        def turned(g):
            return sum((hi - lo + 3) // 4 for lo, hi in TAILS[:g + 1])

        block = ctx.enter_context(nc.Block())

        @block.sync
        def _(sp):
            for i, (a, b) in enumerate(PATCH_LOADS):
                if i == 2:
                    sp.dma_start(emb_sb[:, :, :], emb_in).then_inc(ld_emb, 16)
                    sp.dma_start(wqkv_sb[:, :, :], wqkv).then_inc(ld_wqkv, 16)
                    sp.dma_start(bqkv_sb[:, :], bqkv).then_inc(ld_wqkv, 16)
                sp.dma_start(patch_sb[:, a:b, :], patch_in[:, a:b, :]).then_inc(ld_patch[i], 16)
            sp.dma_start(wo_rows[:, :, :, :], wo_rows_in).then_inc(ld_ff, 16)
            sp.dma_start(wo_sb[:, :, 0:D], wo).then_inc(ld_wo, 16)
            sp.dma_start(wout_sb[:, :], wout).then_inc(ld_wo, 16)
            sp.dma_start(parts_sb[:, :], parts).then_inc(ld_wo, 16)
            results, kept_results = 0, 0
            for _, tiles in ADDS:
                if tiles in BY_VECTOR:
                    results += 1
                    sp.wait_ge(res_ready, results)
                else:
                    kept_results += 1
                    sp.wait_ge(kept, kept_results)
                a, m = tiles[0], rows(tiles[0])
                sp.dma_start(out[0:m, a:a + len(tiles), :], h2[0:m, a:a + len(tiles), 0:D]).then_inc(stored, 16)
            sp.wait_ge(stored, 16 * len(ADDS))

        @block.gpsimd
        def _(pool):
            nc.gpsimd.memset(expo[:, :], -0.5).then_inc(expo_set, 1)
            nc.gpsimd.memset(mv1[:, :, :], 0.0).then_inc(small_set, 1)
            nc.gpsimd.memset(mv2[:, :, :], 0.0).then_inc(small_set, 1)
            nc.gpsimd.memset(h2[:, IMAGES[0]:IMAGES[-1] + 1, D:DX], 0.0).then_inc(small_set, 1)
            nc.gpsimd.memset(co[:, :, 0:1], 0.0).then_inc(small_set, 1)
            nc.gpsimd.memset(kv_i[:, :, 0:1], 0.0).then_inc(pads_set, 1)
            nc.gpsimd.memset(average[:, :], 1.0 / D).then_inc(average_set, 1)
            pool.wait_ge(expo_set, 1)

            def sum_offsets():
                pool.wait_ge(ld_emb, 16)
                nc.gpsimd.tensor_tensor(emb_sb[:, 0, :], emb_sb[:, 0, :], emb_sb[:, 1, :],
                                        ALU.add).then_inc(emb_summed, 1)

            def inverse_deviation(rs, raised, mv, tiles, eps_sem, rstd_sem, count):
                nc.gpsimd.tensor_scalar(raised[:, tiles], mv[:, tiles, 1], EPS, None, ALU.add).then_inc(eps_sem, 1)
                pool.wait_ge(eps_sem, count)
                nc.gpsimd.tensor_tensor(rs[:, tiles], raised[:, tiles], expo[:, tiles], ALU.pow).then_inc(rstd_sem, 1)

            for i, tiles in enumerate(RUNS):
                pool.wait_ge(moments1, tiles[-1] + 1)
                inverse_deviation(rs1, dev1, mv1, slice(tiles[0], tiles[-1] + 1), eps1, rstd1, i + 1)
                if i == 0:
                    sum_offsets()
            pool.wait_ge(ld_ident, 16)
            nc.gpsimd.tensor_copy(ident_r[:, :], ident[:, :]).then_inc(ident_r_set, 1)
            pool.wait_ge(rstd1, len(RUNS))
            nc.gpsimd.tensor_tensor(dev1[:, :], dev1[:, :], rs1[:, :], ALU.mult).then_inc(dev_ready, 1)

            def befores():
                pool.wait_ge(unit_out, out_of_bank(("qkv", "im", "v")))
                nc.gpsimd.tensor_copy(kv_x[:, :, :, 0], kv_i[:, :, IMG::IMG]).then_inc(befores_set, 1)

            def products(r, half):
                pool.wait_ge(unit_out, out_of_bank(("qkv", r, ("q", "qn")[half])))
                for w in range(2):
                    o, q, k = qk_operands(r, half, w)
                    nc.gpsimd.tensor_tensor(o, q, k, ALU.mult).then_inc(qk_ready[r], 1)

            def head_mask(m):
                return head_cols[:, :].unsqueeze(1).unsqueeze(3).broadcast_to([HALF, 4, HH, m])

            def spread_images():
                for p in range(4):
                    nc.gpsimd.tensor_tensor(
                        spread_i[:, p],
                        strided(kv_i[:, p, 1:2], [(IMG, B), (0, HH), (STRIDE, KI)]),
                        head_cols[:, :].unsqueeze(1).unsqueeze(3).broadcast_to([HALF, B, HH, KI]),
                        ALU.mult).then_inc(spread_ready, 1)

            def spread_image_keys(b):
                nc.gpsimd.tensor_tensor(
                    spread_x[:, b, :, :, 0:KI],
                    strided(kv_i[:, 0, 1 + b * IMG:2 + b * IMG], [(1 + B * IMG, 4), (0, HH), (STRIDE, KI)]),
                    head_mask(KI), ALU.mult).then_inc(spread_ready, 1)

            def spread_text_keys(b):
                first_text = STRIDE * KI - IMG
                nc.gpsimd.tensor_tensor(
                    spread_x[:, b, :, :, KI:KT],
                    strided(kv_x[:, 0, b, 1 + first_text:2 + first_text],
                            [(B * SLOTS, 4), (0, HH), (STRIDE, KT - KI)]),
                    head_mask(KT - KI), ALU.mult).then_inc(spread_ready, 1)

            def normalise(n):
                m, k = rows(n), keys(n)
                pool.wait_ge(inv_ready, n + 1)
                s = scores(sc[:, n % RING, :], n)
                nc.gpsimd.tensor_tensor(bandp[0:m, n].rearrange("p w h -> p h w"), s[:, :, k:k + 2],
                                        per_head(rsm[0:m, n, :], 2), ALU.mult).then_inc(bandp_ready, 1)
                if TILES[n][0] == "txt":
                    nc.gpsimd.tensor_tensor(ps[0:m, n % RING].rearrange("p g (h k) -> p (g h) k", h=HH), s[:, :, 0:k],
                                            per_head(rsm[0:m, n, :], k), ALU.mult).then_inc(p_ready, 1)
                else:
                    b = TILES[n][2]
                    for half in range(2):
                        src = half_heads(s, half, 0, k).rearrange("p h (b k) -> p b h k", b=b)
                        r = rsm[0:m, n, half * HH:(half + 1) * HH].unsqueeze(1).unsqueeze(3)
                        nc.gpsimd.tensor_tensor(
                            ps[0:m, n % RING, half, 0:HH * k].rearrange("p (b h k) -> p b h k", b=b, h=HH), src,
                            r.broadcast_to([m, b, HH, KI]), ALU.mult).then_inc(p_ready, 1)

            def band_sum(n):
                pool.wait_ge(band_parts, n + 1)
                nc.gpsimd.tensor_tensor(bandv[:, n % RING, 1, :, 0:rows(n)], bandv[:, n % RING, 1, :, 0:rows(n)],
                                        bandv[:, n % RING, 0, :, 0:rows(n)], ALU.add).then_inc(band_ready, 1)

            pool.wait_ge(ld_heads, 16)
            pool.wait_ge(pads_set, 1)
            pool.wait_ge(unit_out, out_of_bank(("qkv", "x0", "v")))
            for b in range(4):
                spread_text_keys(b)
            befores()
            for b in range(4):
                spread_image_keys(b)
            spread_images()
            for s in range(STEPS):
                if 0 <= s - LAG_VALUES < N:
                    band_sum(s - LAG_VALUES)
                if s < N:
                    normalise(s)
                for what, *of in PREPARE_AT.get(s, []):
                    if what == "spread":
                        i = of[0]
                        pool.wait_ge(unit_out, out_of_bank(("qkv", "x1", "v")))
                        spread_text_keys(i)
                        spread_image_keys(i)
                    else:
                        pool.wait_ge(befores_set, 1)
                        products(*of)
                for g, (lo, hi) in enumerate(SCALES):
                    if s == hi - 1 + LAG_PROJECT:
                        pool.wait_ge(moments2, hi)
                        inverse_deviation(rs2, rs2, mv2, slice(lo, hi), eps2, rstd2, g + 1)

        @block.scalar
        def _(act):
            def load_text(i):
                a, b, k = TEXT_RUNS[i]
                act.dma_start(h[:, a:a + k, 0:D], txt[:, b:b + k, :]).then_inc(ld_txt[i], 16)

            load_text(0)
            act.dma_start(ident[:, :], ident_d).then_inc(ld_ident, 16)
            act.dma_start(head_cols[:, :], head_cols_d).then_inc(ld_heads, 16)
            act.dma_start(identb[:, :], identb_d).then_inc(ld_masks, 16)
            act.dma_start(mask_txt[:, :], mask_txt_d).then_inc(ld_masks, 16)
            load_text(1)
            act.dma_start(mask_img[:, :], mask_img_d).then_inc(ld_masks, 16)
            act.dma_start(mask_end[:, :], mask_end_d).then_inc(ld_masks, 16)

            def xnT_out(i):
                act.wait_ge(xnT_psum, i + 1)
                dst, src = turned_tokens(i, 0)
                nc.scalar.activation(dst, src, ACT.Copy).then_inc(xnT_hi, 1)

            def unit_evict(u):
                what = UNITS[u]
                act.wait_ge(unit_done, u + 1)
                if what[0] == "vbd":
                    _, n, count = what
                    k = HH * keys(n)
                    nc.scalar.activation(vbd[0:k, n:n + count, :, :].rearrange("p t g f -> p (t g f)"),
                                         R[u % 3][0:k, 0:count * D], ACT.Copy).then_inc(unit_out, 1)
                    return
                if what[0] == "gain":
                    nc.scalar.activation(wo_sb[:, :, D:DX], R[u % 3][0:HALF + 1, 0:2 * NODES]
                                         .rearrange("p (g n) -> p g n", g=2), ACT.Copy).then_inc(unit_out, 1)
                    return
                if what[0] == "logits":
                    _, n, count = what
                    act.wait_ge(dev_ready, 1)
                    for i in range(count):
                        m = rows(n + i)
                        last = nc.scalar.activation(h[0:m, n + i, D:DX], R[u % 3][0:m, i * NODES:(i + 1) * NODES],
                                                    ACT.Copy, scale=dev1[0:m, n + i:n + i + 1])
                    last.then_inc(unit_out, 1)
                    return
                _, r, group = what
                bank, b = R[u % 3], 4 * RANGES.index(r)
                if group == "qn":
                    rest = bank[LG:LG + NODES, :]
                    if r == "im":
                        nc.scalar.activation(lgT_i[LG:, :], rest[:, 0:B * IMG], ACT.Copy)
                    else:
                        nc.scalar.activation(lgT_x[LG:, b:b + 4, :].rearrange("p b t -> p (b t)"), rest, ACT.Copy)
                place = 0
                for half, first, size in PIECES[group]:
                    features, part = slice(first, first + size), half_index(half)
                    if r == "im":
                        dst = q_i[features, part] if part < 2 else kv_i[features, part - 2, 1:]
                        src = bank[place:place + size, 0:B * IMG]
                    else:
                        dst = q_x[features, part, b:b + 4] if part < 2 else kv_x[features, part - 2, b:b + 4, 1:]
                        src = bank[place:place + size, :].rearrange("p (b t) -> p b t", b=4)
                    g = GROUPS.index(group)
                    last = nc.scalar.activation(dst, src, ACT.Identity, bias=bqkv_sb[place:place + size, g:g + 1])
                    place += size
                last.then_inc(unit_out, 1)

            def exponent(n):
                act.wait_ge(sc_shifted, n + 1)
                s = sc[0:rows(n), n % RING, 0:H * (keys(n) + 2)]
                nc.scalar.activation(s, s, ACT.Exp, scale=SCALE).then_inc(sc_exp, 1)

            def repeat_band(n):
                m = rows(n)
                act.wait_ge(bandp_ready, n + 1)
                nc.scalar.activation(pb[0:m, n % RING].rearrange("p w (h f) -> p (w h) f", h=H),
                                     bandp[0:m, n].rearrange("p w h -> p (w h)").unsqueeze(2)
                                     .broadcast_to([m, 2 * H, HD]), ACT.Copy).then_inc(pb_ready, 1)

            def pT_out(n):
                k = HH * keys(n)
                act.wait_ge(p_psum, n + 1)
                nc.scalar.activation(pT[0:k, n % RING, :, 0:rows(n)], two(B_PT[0:k, :], n),
                                     ACT.Copy).then_inc(pT_ready, 1)

            def h2_out(n):
                m = rows(n)
                act.wait_ge(proj_psum, n + 1)
                if n == IMAGES[0]:
                    act.wait_ge(small_set, 4)
                nc.scalar.activation(h2[0:m, n, :], B_PROJ[0:m, 0:DX], ACT.Copy).then_inc(h2_ready, 1)

            def gelu(g, tiles):
                act.wait_ge(h2_ready, tiles[-1] + 1)
                act.wait_ge(rstd2, g + 1)
                for n in tiles:
                    nc.scalar.activation(gl[:, n, :], h2[:, n, D:DX], ACT.Gelu,
                                         scale=rs2[:, n:n + 1]).then_inc(gelu_ready, 1)

            def coT_out(g):
                lo, hi = TAILS[g]
                for i, a in enumerate(range(lo, hi, 4)):
                    b = min(a + 4, hi)
                    act.wait_ge(coT_psum, turned(g - 1) + i + 1)
                    nc.scalar.activation(coT[:, a:b, :].rearrange("p n t -> p (n t)"),
                                         co_banks(g)[i][0:STACK, 0:(b - a) * 128], ACT.Copy).then_inc(coT_ready, 1)

            act.wait_ge(ld_wqkv, 32)
            nc.scalar.activation(wqkv_hi[:, :, :], wqkv_sb[:, :, :], ACT.Copy).then_inc(w_hi, 1)
            for i in range(2):
                xnT_out(i)
            for u in FRONT:
                if u[0] == "turn":
                    xnT_out(u[1])
                elif u[0] not in VECTOR_READS:
                    unit_evict(UNITS.index(u))
            for s in range(STEPS):
                if s < N and leading(s):
                    exponent(s)
                if 0 <= s - LAG_VALUES < N:
                    pT_out(s - LAG_VALUES)
                for u in leading(s):
                    unit_evict(UNITS.index(u))
                if s < N and not leading(s):
                    exponent(s)
                if 0 <= s - LAG_PROJECT < N:
                    h2_out(s - LAG_PROJECT)
                if s < N:
                    repeat_band(s)
                for u in UNITS_AT.get(s, [])[len(leading(s)):]:
                    if u[0] not in VECTOR_READS:
                        unit_evict(UNITS.index(u))
                if s == N - 1:
                    gelu(0, range(1))
                if s == N:
                    gelu(0, range(1, SCALES[0][1]))
            gelu(1, range(*SCALES[1]))
            gelu(2, range(*SCALES[2]))

            def keep(adds):
                for i in adds:
                    _, tiles = ADDS[i]
                    a, k, m = tiles[0], len(tiles), rows(tiles[0])
                    b, c = ff_place(a)
                    act.wait_ge(ff_psum, i + 1)
                    nc.scalar.activation(h2[0:m, a:a + k, 0:D], b[0:m, c:c + k * D].rearrange("p (t f) -> p t f", t=k),
                                         ACT.Copy).then_inc(kept, 1)

            coT_out(0)
            keep([0, 1])
            coT_out(1)
            keep([3, 5])

        @block.vector
        def _(dve):
            def moments(src, st, mv, n, stats_sem, moments_sem, count):
                m = rows(n)
                nc.vector.bn_stats(st[0:m, n, :], src[0:m, n, 0:D]).then_inc(stats_sem, 1)
                dve.wait_ge(stats_sem, count)
                nc.vector.bn_aggr(mv[0:m, n, :], st[0:m, n, :]).then_inc(moments_sem, 1)

            def xn_out(n):
                m = rows(n)
                nc.vector.tensor_scalar(xn[0:m, n, :], h[0:m, n, 0:D], mv1[0:m, n, 0:1], rs1[0:m, n:n + 1],
                                        ALU.subtract, ALU.mult).then_inc(xn_ready, 1)

            nc.vector.memset(idle[:, :], 0.0).then_inc(idle_set, 1)
            nc.vector.memset(oT[HALF:HALF + 1, :, :, :], 1.0).then_inc(ones_set, 1)
            dve.wait_ge(small_set, 4)

            def moments_of(tiles):
                for n in tiles:
                    if TILES[n][0] == "txt":
                        dve.wait_ge(ld_txt[int(n >= TEXT_RUNS[1][0])], 16)
                    else:
                        dve.wait_ge(emb_out, IMAGES.index(n) + 1)
                    moments(h, st1, mv1, n, stats1, moments1, n + 1)

            def normalise_run(i):
                dve.wait_ge(rstd1, i + 1)
                for n in RUNS[i]:
                    xn_out(n)

            def xnT_rest(i):
                dve.wait_ge(xnT_hi, i + 1)
                dst, src = turned_tokens(i, 1)
                nc.vector.tensor_tensor(dst, src, turned_tokens(i, 0)[0], ALU.subtract).then_inc(xnT_lo, 1)

            moments_of(RUNS[0])
            normalise_run(0)
            dve.wait_ge(ld_wqkv, 32)
            dve.wait_ge(w_hi, 1)
            nc.vector.tensor_tensor(wqkv_lo[:, :, :], wqkv_sb[:, :, :], wqkv_hi[:, :, :], ALU.subtract).then_inc(w_lo, 1)
            xnT_rest(0)
            xnT_rest(1)
            for i, n in enumerate(IMAGES):
                m = rows(n)
                dve.wait_ge(emb_done, i + 1)
                dve.wait_ge(emb_summed, 1)
                nc.vector.tensor_tensor(h[0:m, n, 0:D], B_EMB[i][0:m, 0:D], emb_sb[0:m, 0, :],
                                        ALU.add).then_inc(emb_out, 1)
                moments_of([n])
            moments_of(RUNS[2][:2])
            normalise_run(1)
            moments_of(RUNS[2][2:])
            for i in (2, 3, 4):
                xnT_rest(i)
            normalise_run(2)
            u = UNITS.index(("means",))
            dve.wait_ge(unit_done, u + 1)
            nc.vector.tensor_tensor(win_centred[:, :, :], wqkv_sb[:, :, 3 * D:WX],
                                    R[u % 3][0:HALF, 0:NODES].unsqueeze(1).broadcast_to([HALF, 2, NODES]),
                                    ALU.subtract).then_inc(centred, 1)
            dve.wait_ge(ld_wo, 48)
            nc.vector.tensor_copy(wout_hi[:, :], wout_sb[:, :]).then_inc(wout_split, 1)
            dve.wait_ge(wout_split, 1)
            nc.vector.tensor_tensor(wout_lo[:, :], wout_sb[:, :], wout_hi[:, :], ALU.subtract).then_inc(wout_split, 1)
            nc.vector.tensor_scalar(wout_mix[:, :], wout_hi[:, :], parts_sb[:, 0:1], None,
                                    ALU.mult).then_inc(wout_split, 1)
            dve.wait_ge(wout_split, 3)
            nc.vector.scalar_tensor_tensor(wout_stack[:, :], wout_lo[:, :], parts_sb[:, 1:2], wout_mix[:, :],
                                           ALU.mult, ALU.add).then_inc(wout_ready, 1)
            for i in (5, 6):
                xnT_rest(i)
            dve.wait_ge(pads_set, 1)
            for half, group in enumerate(("q", "qn")):
                dve.wait_ge(unit_out, out_of_bank(("qkv", "x0", group)))
                for w in range(2):
                    if w == 1:
                        dve.wait_ge(befores_set, 1)
                    o, q, k = qk_operands("x0", half, w)
                    nc.vector.tensor_tensor(o, q, k, ALU.mult).then_inc(qk_ready["x0"], 1)

            def sum_dots(n):
                m = rows(n)
                u = UNITS.index(("dots", n))
                dve.wait_ge(unit_done, u + 1)
                nc.vector.tensor_reduce(dots[0:m, n].rearrange("p w h -> p (w h)"),
                                        R[u % 3][0:m, 0:2 * D].rearrange("p (g f) -> p g f", f=HD),
                                        AX_X, ALU.add).then_inc(dots_ready, 1)

            def add_dots(n):
                dve.wait_ge(sc_psum, n + 1)
                dve.wait_ge(dots_ready, n + 1)
                band = scores(B_SC[:, :], n)[:, :, keys(n):keys(n) + 2]
                nc.vector.tensor_tensor(band, band, dots[0:rows(n), n].rearrange("p w h -> p h w"),
                                        ALU.add).then_inc(dots_added, 1)

            def maxima(n):
                dve.wait_ge(dots_added, n + 1)
                nc.vector.tensor_reduce(mx[0:rows(n), n, :], scores(B_SC[:, :], n), AX_X, ALU.max).then_inc(max_ready, 1)

            def shift(n):
                dve.wait_ge(max_ready, n + 1)
                nc.vector.tensor_tensor(scores(sc[:, n % RING, :], n), scores(B_SC[:, :], n),
                                        per_head(mx[0:rows(n), n, :], keys(n) + 2),
                                        ALU.subtract).then_inc(sc_shifted, 1)

            def sums(n):
                m = rows(n)
                dve.wait_ge(sc_exp, n + 1)
                nc.vector.tensor_reduce(sm[0:m, n, :], scores(sc[:, n % RING, :], n), AX_X, ALU.add).then_inc(sum_ready, 1)
                dve.wait_ge(sum_ready, n + 1)
                nc.vector.reciprocal(rsm[0:m, n, :], sm[0:m, n, :]).then_inc(inv_ready, 1)

            def band_products(n):
                m = rows(n)
                dve.wait_ge(p_psum, n + 1)
                p = B_BAND[0:HALF, :].rearrange("p (w g t) -> p w g t", w=2, g=2)[:, :, :, 0:m]
                nc.vector.tensor_tensor(bandv[:, n % RING, :, :, 0:m], p, values(n), ALU.mult).then_inc(band_parts, 1)

            def attended(n):
                m = rows(n)
                dve.wait_ge(pv_psum, n + 1)
                dve.wait_ge(band_ready, n + 1)
                nc.vector.tensor_tensor(oT[0:HALF, n % RING, :, 0:m], two(B_PV[0:HALF, :], n),
                                        bandv[:, n % RING, 1, :, 0:m],
                                        ALU.add).then_inc(oT_ready, 1)

            def statistics_after(n):
                m = rows(n)
                dve.wait_ge(h2_ready, n + 1)
                nc.vector.bn_stats(st2[0:m, n, :], h2[0:m, n, 0:D]).then_inc(stats2, 1)

            def moments_after(n):
                m = rows(n)
                dve.wait_ge(stats2, n + 1)
                nc.vector.bn_aggr(mv2[0:m, n, :], st2[0:m, n, :]).then_inc(moments2, 1)

            ticks = [0]

            def tick(ins):
                ticks[0] += 1
                ins.then_inc(tree, 1)
                dve.wait_ge(tree, ticks[0])

            def path(g):
                lo, hi = TAILS[g]
                k = hi - lo
                dve.wait_ge(h2_ready, hi)
                for right, compare in enumerate((ALU.is_le, ALU.is_gt)):
                    nc.vector.tensor_scalar(on[:, lo:hi, 1 + right:21:2], h2[:, lo:hi, D:D + 10], 0.0, None,
                                            compare).then_inc(tree, 1)
                    ticks[0] += 1
                dve.wait_ge(tree, ticks[0])

                def children(first, count):
                    parents = on[:, lo:hi, first:first + count].unsqueeze(3).broadcast_to([128, k, count, 2])
                    o = on[:, lo:hi, 2 * first + 1:2 * (first + count) + 1].rearrange("p t (n s) -> p t n s", s=2)
                    tick(nc.vector.tensor_tensor(o, o, parents, ALU.mult))

                children(1, 2)
                children(3, 4)
                children(7, 3)

            def coefficients(g):
                lo, hi = TAILS[g]
                k = hi - lo
                dve.wait_ge(gelu_ready, hi)
                if g == 0:
                    dve.wait_ge(small_set, 4)
                nc.vector.tensor_tensor(co[:, lo:hi, 1:21].rearrange("p t (n s) -> p t n s", s=2),
                                        on[:, lo:hi, 1:21].rearrange("p t (n s) -> p t n s", s=2),
                                        gl[:, lo:hi, 0:10].unsqueeze(3).broadcast_to([128, k, 10, 2]),
                                        ALU.mult).then_inc(co_parts, 1)
                nc.vector.tensor_tensor(co[:, lo:hi, ROW_LEVEL5:ROW_LEVEL6], on[:, lo:hi, 10:21], gl[:, lo:hi, 10:21],
                                        ALU.mult).then_inc(co_parts, 1)
                nc.vector.tensor_tensor(co[:, lo:hi, ROW_LEVEL6:ROW_REST], on[:, lo:hi, 10:15],
                                        gl[:, lo:hi, 20:21].broadcast_to([128, k, 5]),
                                        ALU.mult).then_inc(co_parts, 1)
                nc.vector.tensor_scalar(co[:, lo:hi, ROW_REST], gl[:, lo:hi, 20], 5.0, None,
                                        ALU.mult).then_inc(co_parts, 1)

            def high_parts(g):
                high, _, whole = coefficient_parts(g)
                dve.wait_ge(co_parts, 4 * (g + 1))
                nc.vector.tensor_copy(high, whole).then_inc(co_high, 1)

            def low_parts(g):
                high, low, whole = coefficient_parts(g)
                dve.wait_ge(co_high, g + 1)
                nc.vector.tensor_tensor(low, whole[:, :, 0, :], high[:, :, 0, :], ALU.subtract).then_inc(co_ready, 1)

            def results():
                for i, (_, tiles) in enumerate(ADDS):
                    if tiles in BY_VECTOR:
                        a, k, m = tiles[0], len(tiles), rows(tiles[0])
                        b, c = ff_place(a)
                        dve.wait_ge(ff_psum, i + 1)
                        nc.vector.tensor_tensor(h2[0:m, a:a + k, 0:D], h2[0:m, a:a + k, 0:D],
                                                b[0:m, c:c + k * D].rearrange("p (t f) -> p t f", t=k),
                                                ALU.add).then_inc(res_ready, 1)

            sum_dots(0)
            for s in range(N):
                add_dots(s)
                if s >= 3:
                    statistics_after(s - 3)
                maxima(s)
                if s >= 3:
                    moments_after(s - 3)
                shift(s)
                if s >= LAG_VALUES:
                    band_products(s - LAG_VALUES)
                sums(s)
                if s < N - 1:
                    sum_dots(s + 1)
                if s >= LAG_VALUES:
                    attended(s - LAG_VALUES)
            statistics_after(N - 3)
            moments_after(N - 3)
            path(0)
            band_products(N - 1)
            statistics_after(N - 2)
            moments_after(N - 2)
            attended(N - 1)
            coefficients(0)
            statistics_after(N - 1)
            high_parts(0)
            moments_after(N - 1)
            low_parts(0)
            path(1)
            coefficients(1)
            high_parts(1)
            low_parts(1)
            results()

        @block.tensor
        def _(pe):
            def xn_transposes(i):
                if i >= len(B_LN):
                    pe.wait_ge(xnT_lo, i - len(B_LN) + 1)
                for j, n in enumerate(TURNS[i]):
                    m = rows(n)
                    pe.wait_ge(xn_ready, n + 1)
                    o = two(B_LN[i % len(B_LN)][0:HALF, 256 * j:256 * j + 256], n)
                    for half in range(2):
                        last = nc.tensor.transpose(o[:, half, :], xn[0:m, n, half * HALF:(half + 1) * HALF],
                                                   ident[0:m, 0:m])
                last.then_inc(xnT_psum, 1)

            def unit(u):
                what = UNITS[u]
                o = R[u % 3]
                if u == 2:
                    pe.wait_ge(emb_out, len(IMAGES))
                elif u >= 3 and UNITS[u - 3][0] == "means":
                    pe.wait_ge(centred, 1)
                elif u >= 3 and UNITS[u - 3][0] == "dots":
                    pe.wait_ge(dots_ready, UNITS[u - 3][1] + 1)
                elif u >= 3:
                    pe.wait_ge(unit_out, out_of_bank(UNITS[u - 3]))
                if what[0] == "qkv":
                    _, r, group = what
                    pe.wait_ge(xnT_lo, {"x0": 2, "im": 5, "x1": 7}[r])
                    first = 128 * GROUPS.index(group)
                    cols = slice(first, min(first + 128, WX))
                    dst = o[0:cols.stop - cols.start, 0:B * IMG] if r == "im" else o[0:cols.stop - cols.start, :]
                    products = [(half, w, x) for half in range(2)
                                for w, x in ((wqkv_hi, 0), (wqkv_hi, 1), (wqkv_lo, 0))]
                    for i, (half, w, x) in enumerate(products):
                        if r == "im":
                            src = xnT_i[x][:, half]
                        else:
                            b = 4 * RANGES.index(r)
                            src = xnT_x[x][:, half, b:b + 4].rearrange("p b t -> p (b t)")
                        last = nc.tensor.matmul(dst, w[:, half, cols], src,
                                                start=(i == 0), stop=(i == len(products) - 1))
                elif what[0] == "means":
                    pe.wait_ge(average_set, 1)
                    for half in range(2):
                        last = nc.tensor.matmul(o[0:HALF, 0:NODES], average[:, :], wqkv_sb[:, half, 3 * D:WX],
                                                start=(half == 0), stop=(half == 1))
                elif what[0] == "gain":
                    pe.wait_ge(centred, 1)
                    pe.wait_ge(ld_ff, 16)
                    for half in range(2):
                        for part in range(2):
                            last = nc.tensor.matmul(o[0:HALF + 1, half * NODES:(half + 1) * NODES],
                                                    wo_rows[:, part, half, :], win_centred[:, part, :],
                                                    start=(part == 0), stop=(part == 1))
                elif what[0] == "logits":
                    _, n, count = what
                    pe.wait_ge(unit_out, out_of_bank(("qkv", range_of(n), "qn")))
                    for i in range(count):
                        last = nc.tensor.transpose(o[0:rows(n + i), i * NODES:(i + 1) * NODES],
                                                   tokens(lgT_x[LG:], lgT_i[LG:], n + i),
                                                   ident[LG:LG + NODES, LG:LG + NODES])
                elif what[0] == "dots":
                    n = what[1]
                    pe.wait_ge(qk_ready[range_of(n)], 4)
                    for w in range(2):
                        for half in range(2):
                            c = w * D + half * HALF
                            last = nc.tensor.transpose(o[0:rows(n), c:c + HALF],
                                                       tokens(qk_x[:, w, half], qk_i[:, w, half], n),
                                                       ident[0:HALF, 0:HALF])
                else:
                    _, n, count = what
                    k = HH * keys(n)
                    pe.wait_ge(spread_ready, spreads(n + count - 1))
                    for i in range(count):
                        for half in range(2):
                            c = i * D + half * HALF
                            last = nc.tensor.transpose(o[0:k, c:c + HALF], block_diagonal(n + i, 2 + half),
                                                       ident[0:HALF, 0:HALF])
                last.then_inc(unit_done, 1)

            def block_diagonal(n, part):
                _, first, count = TILES[n]
                if TILES[n][0] == "txt":
                    return spread_x[:, first, part].rearrange("p h k -> p (h k)")
                return spread_i[:, part, first:first + count].rearrange("p b h k -> p (b h k)")

            def image_cols(i):
                _, first, _ = TILES[IMAGES[i]]
                return slice(first * IMG, first * IMG + rows(IMAGES[i]))

            pe.wait_ge(idle_set, 1)
            for _ in range(WARM_UP):
                nc.tensor.matmul(B_EMB[0][:, 0:256], idle[:, 0:128], idle[:, :], start=True, stop=True)
            for load, (a, b) in enumerate(PATCH_LOADS):
                if load == 2:
                    pe.wait_ge(ld_ident, 16)
                    for i in range(2):
                        xn_transposes(i)
                pe.wait_ge(ld_patch[load], 16)
                for k in range(a, b):
                    for i, n in enumerate(IMAGES):
                        last = nc.tensor.matmul(B_EMB[i][0:rows(n), 0:D], patch_sb[:, k, image_cols(i)],
                                                patch_sb[:, k, B * IMG:], start=(k == 0), stop=(k == KC - 1))
                        if k == KC - 1:
                            last.then_inc(emb_done, 1)

            pe.wait_ge(w_hi, 1)
            pe.wait_ge(w_lo, 1)
            for u in FRONT:
                if u[0] == "turn":
                    xn_transposes(u[1])
                else:
                    unit(UNITS.index(u))

            def make_scores(n):
                m, k = rows(n), keys(n)
                if n:
                    pe.wait_ge(sc_shifted, n)
                pe.wait_ge(unit_out, out_of_bank(("qkv", range_of(n), "qn")))
                pe.wait_ge(spread_ready, spreads(n))
                mask = mask_txt if TILES[n][0] == "txt" else mask_img
                if TILES[n][0] == "img" and TILES[n][2] != IB:
                    mask = mask_end
                o = scores(B_SC[:, :], n)
                nc.tensor.matmul(B_SC[0:m, 0:H * (k + 2)], identb[0:m, 0:m], mask[0:m, 0:H * (k + 2)],
                                 start=True, stop=False, skip_group_check=True)
                for half in range(2):
                    dst = half_heads(o, half, 0, k)
                    if TILES[n][0] == "img":
                        dst = dst.rearrange("p h (b k) -> p b h k", k=KI)
                    last = nc.tensor.matmul(dst, tokens(q_x[:, half], q_i[:, half], n), block_diagonal(n, half),
                                            start=False, stop=(half == 1), skip_group_check=True)
                last.then_inc(sc_psum, 1)

            def turn_probabilities(n):
                m, k = rows(n), keys(n)
                pe.wait_ge(p_ready, normalised(n))
                pe.wait_ge(pb_ready, n + 1)
                if n:
                    pe.wait_ge(pT_ready, n)
                    pe.wait_ge(band_parts, n)
                for half in range(2):
                    nc.tensor.transpose(two(B_PT[0:HH * k, :], n)[:, half, :], ps[0:m, n % RING, half, 0:HH * k],
                                        ident[0:m, 0:m])
                bnd = B_BAND[0:HALF, :].rearrange("p (w g t) -> p w g t", w=2, g=2)
                for w in range(2):
                    for half in range(2):
                        last = nc.tensor.transpose(bnd[:, 1 - w, half, 0:m],
                                                   pb[0:m, n % RING, w, half * HALF:(half + 1) * HALF], ident[0:m, 0:m])
                last.then_inc(p_psum, 1)

            def weigh_values(n):
                k = HH * keys(n)
                pe.wait_ge(pT_ready, n + 1)
                pe.wait_ge(unit_out, out_of_bank(vbd_unit(n)))
                if n:
                    pe.wait_ge(oT_ready, n)
                for half in range(2):
                    last = nc.tensor.matmul(two(B_PV[0:HALF, :], n)[:, half, :], vbd[0:k, n, half, :],
                                            pT[0:k, n % RING, half, 0:rows(n)], start=True, stop=True)
                last.then_inc(pv_psum, 1)

            def project(n):
                m = rows(n)
                if n:
                    pe.wait_ge(h2_ready, n)
                pe.wait_ge(unit_out, out_of_bank(logits_unit(n)))
                nc.tensor.matmul(B_PROJ[0:m, 0:DX], ident[0:m, 0:m], h[0:m, n, :], start=True, stop=False)
                pe.wait_ge(oT_ready, n + 1)
                for half in range(2):
                    kk = HALF + 1 if half == 0 else HALF
                    last = nc.tensor.matmul(B_PROJ[0:m, 0:DX], oT[0:kk, n % RING, half, 0:m], wo_sb[0:kk, half, :],
                                            start=False, stop=(half == 1))
                last.then_inc(proj_psum, 1)

            def turn_coefficients(g):
                lo, hi = TAILS[g]
                pe.wait_ge(co_ready, g + 1)
                if g:
                    pe.wait_ge(coT_ready, turned(g - 1))
                for i, a in enumerate(range(lo, hi, 4)):
                    for n in range(a, min(a + 4, hi)):
                        last = nc.tensor.matmul(co_banks(g)[i][0:STACK, (n - a) * 128:(n - a + 1) * 128],
                                                co_stack[:, n].rearrange("p s r -> p (s r)"), ident_r[:, :],
                                                start=True, stop=True)
                    last.then_inc(coT_psum, 1)

            def residuals(g):
                for n in [n for tiles in OUT_SETS[g] if tiles not in BY_VECTOR for n in tiles]:
                    b, c = ff_place(n)
                    nc.tensor.matmul(b[0:rows(n), c:c + D], ident[0:rows(n), 0:rows(n)], h2[0:rows(n), n, 0:D],
                                     start=(c == 0), stop=False, skip_group_check=True)

            def tree_output(g):
                pe.wait_ge(coT_ready, turned(g))
                for tiles in OUT_SETS[g]:
                    for n in tiles:
                        b, c = ff_place(n)
                        last = nc.tensor.matmul(b[0:rows(n), c:c + D], coT[:, n, 0:rows(n)], wout_stack[:, :],
                                                start=(tiles in BY_VECTOR), stop=True, skip_group_check=True)
                    last.then_inc(ff_psum, 1)

            pe.wait_ge(ld_masks, 64)
            for s in range(STEPS):
                if s < N:
                    make_scores(s)
                for u in leading(s):
                    unit(UNITS.index(u))
                if 0 <= s - LAG_VALUES < N:
                    turn_probabilities(s - LAG_VALUES)
                if 0 <= s - LAG_PROJECT < N:
                    if s == LAG_PROJECT:
                        pe.wait_ge(ld_wo, 48)
                        pe.wait_ge(ones_set, 1)
                    project(s - LAG_PROJECT)
                if 0 <= s - LAG_VALUES < N:
                    weigh_values(s - LAG_VALUES)
                for u in UNITS_AT.get(s, [])[len(leading(s)):]:
                    unit(UNITS.index(u))
            pe.wait_ge(pT_ready, N)
            pe.wait_ge(band_parts, N)
            residuals(0)
            pe.wait_ge(ident_r_set, 1)
            pe.wait_ge(wout_ready, 1)
            turn_coefficients(0)
            pe.wait_ge(oT_ready, N)
            pe.wait_ge(h2_ready, N)
            residuals(1)
            tree_output(0)
            turn_coefficients(1)
            tree_output(1)


def _constants(np, bf16):
    masked = -1e30

    def score_mask(positions, key_positions):
        m = np.zeros((len(positions), H, len(key_positions) + 2), np.float32)
        for r, (b, i) in enumerate(positions):
            for c, (kb, j) in enumerate(key_positions):
                if kb != b or j > i:
                    m[r, :, c] = masked
            if i % STRIDE == 0:
                m[r, :, -2] = masked
            if i == 0 or (i - 1) % STRIDE == 0:
                m[r, :, -1] = masked
        return m.reshape(len(positions), -1).astype(bf16)

    def image(count):
        return ([(b, i) for b in range(count) for i in range(IMG)],
                [(b, STRIDE * j) for b in range(count) for j in range(KI)])

    return {
        "ident": np.eye(128, dtype=np.float32),
        "identb": np.eye(128).astype(bf16),
        "mask_txt": score_mask([(0, IMG + t) for t in range(TXT)], [(0, STRIDE * j) for j in range(KT)]),
        "mask_img": score_mask(*image(IB)),
        "mask_end": score_mask(*image(TILES[IMAGES[-1]][2])),
        "head_cols": np.kron(np.eye(HH), np.ones((HD, 1))).astype(np.float32),
        "parts": np.repeat(np.array([[1, 0], [1, 0], [0, 1]], np.float32), ROWS, axis=0),
    }


def kernel(x, txt, L0_tok_W_proj, L0_tok_b_proj, L0_tok_cls_token, L0_tok_pos_embedding,
           L0_attn_qkv_w, L0_attn_qkv_b, L0_attn_out_w, L0_attn_out_b,
           L0_ffn_weights_in, L0_ffn_weights_out):
    import ml_dtypes
    import numpy as np
    import concourse.bacc as bacc
    from concourse.bass_utils import run_bass_kernel_spmd

    side = x.shape[1] // 16
    patches = np.asarray(x).reshape(B, side, 16, side, 16, 3).transpose(2, 4, 5, 0, 1, 3).reshape(16 * 16 * 3, B, IMG - 1)
    xp = np.zeros((KC * 128, B, IMG), np.float32)
    xp[:, :, 1:] = patches
    wo = np.zeros((HALF + 1, 2, D), np.float32)
    wo[:HALF] = np.asarray(L0_attn_out_w).T.reshape(2, HALF, D).transpose(1, 0, 2)
    wo[HALF, 0] = np.asarray(L0_attn_out_b)
    emb_base = np.concatenate([np.asarray(L0_tok_cls_token)[0]] + [np.asarray(L0_tok_b_proj)[None]] * (IMG - 1))
    emb = np.stack([emb_base, np.asarray(L0_tok_pos_embedding)], axis=1)
    order = {g: [half_index(half) * HALF + first + i for half, first, size in PIECES[g] for i in range(size)]
             for g in GROUPS}
    biases = np.zeros((128, len(GROUPS)), np.float32)
    for i, g in enumerate(GROUPS):
        biases[:len(order[g]), i] = np.asarray(L0_attn_qkv_b)[order[g]]
    arrays = {
        "patch": np.concatenate([xp.reshape(KC, 128, B * IMG), np.asarray(L0_tok_W_proj).reshape(KC, 128, D)],
                                axis=2).transpose(1, 0, 2),
        "emb": np.tile(emb, (IB, 1, 1)),
        "txt": np.asarray(txt).transpose(1, 0, 2),
        "wqkv": np.concatenate([np.asarray(L0_attn_qkv_w)[sum(order.values(), [])],
                                np.asarray(L0_ffn_weights_in)]).T
        .reshape(2, HALF, WX).transpose(1, 0, 2),
        "bqkv": biases,
        "wo": wo,
        "wo_rows": np.stack([np.concatenate([w.reshape(2, HALF, HALF), b.reshape(2, HALF, 1)], axis=2).transpose(1, 0, 2)
                             for w, b in ((np.asarray(L0_attn_out_w)[:, :HALF], np.asarray(L0_attn_out_b)),
                                          (np.asarray(L0_attn_out_w)[:, HALF:], np.zeros(D, np.float32)))], axis=2),
        "wout": np.tile(np.concatenate([np.asarray(L0_ffn_weights_out)]
                                       + [np.asarray(L0_ffn_weights_out)[-1:]] * (ROWS - NODES)), (3, 1)),
        **_constants(np, ml_dtypes.bfloat16),
    }
    arrays = {f"in_{name}": np.ascontiguousarray(a) for name, a in arrays.items()}
    nc = bacc.Bacc("TRN2", target_bir_lowering=False, num_devices=1)
    aps = [nc.dram_tensor(name, a.shape, mybir.dt.from_np(a.dtype), kind="ExternalInput").ap()
           for name, a in arrays.items()]
    aps.append(nc.dram_tensor("out", (128, N, D), F32, kind="ExternalOutput").ap())
    build(nc, *aps)
    tiles = run_bass_kernel_spmd(nc, [arrays], core_ids=[0]).results[0]["out"]
    result = np.empty((B, S, D), np.float32)
    for n, (kind, first, count) in enumerate(TILES):
        if kind == "txt":
            result[first, IMG:] = tiles[:, n]
        else:
            result[first:first + count, :IMG] = tiles[:rows(n), n].reshape(count, IMG, D)
    return result
```
